# Optimizing a Trainium2 kernel written in Bass

```python
import numpy as np
import jax
import jax.numpy as jnp

def _softmax(x, axis=-1):
    return jax.nn.softmax(x, axis=axis)

def _gelu(x):
    return jax.nn.gelu(x, approximate=True)

def _silu(x):
    return jax.nn.silu(x)

def _sigmoid(x):
    return jax.nn.sigmoid(x)

def _layernorm(x, axis=-1, eps=1e-05):
    m = jnp.mean(x, axis=axis, keepdims=True)
    v = jnp.var(x, axis=axis, keepdims=True)
    return (x - m) / jnp.sqrt(v + eps)

def _scatter_add(tgt, idx, src, axis=0):
    return tgt.at[idx].add(src)

def _segment_sum(src, seg, n):
    return jax.ops.segment_sum(src, seg, n)
kernel_name = 'mk_gnn_preln_d2_gnn_r8_e1ab3c'

def setup_inputs(seed: int=0):
    np.random.seed(seed)
    _w = jnp.asarray

    def _rec_inputs():
        import jax
        import jax.numpy as jnp
        _gk = jax.random.key(seed)
        x = -0.0009044 + 1 * jax.random.normal(jax.random.fold_in(_gk, 1), (12500, 32), jnp.float32)
        src = jax.random.randint(jax.random.fold_in(_gk, 2), (200000,), 0, 12500, jnp.int32)
        dst = jnp.minimum((12500 * jax.random.uniform(jax.random.fold_in(_gk, 3), (200000,)) ** 2.0).astype(jnp.int32), 99999)
        _o = jnp.argsort(dst, stable=True)
        src = src[_o]
        dst = dst[_o]
        edge_attr_16 = 0.000254156 + 0.999948 * jax.random.normal(jax.random.fold_in(_gk, 11), (200000, 16), jnp.float32)
        return (x, src, dst, edge_attr_16)
    x, src, dst, edge_attr_16 = _rec_inputs()

    def _L0_gnn_setup():
        import jax, jax.numpy as jnp
        import numpy as np
        N_NODES = 6250
        N_EDGES = 100000
        NODE_D, EDGE_D = (32, 16)
        FLOW_IN, FLOW_H, FLOW_OUT = (2 * NODE_D + EDGE_D, 64, 64)
        NODE_H, NODE_OUT = (64, 32)

        def _mlp(h, W1, b1, W2, b2):
            h = jax.nn.relu(h @ W1 + b1)
            return h @ W2 + b2
        key = jax.random.key(seed)
        ks = jax.random.split(key, 8)
        return {'x': jax.random.normal(ks[0], (N_NODES, NODE_D), dtype=jnp.float32), 'edge_index': jax.random.randint(ks[1], (2, N_EDGES), 0, N_NODES, dtype=jnp.int64), 'edge_attr': jax.random.normal(ks[2], (N_EDGES, EDGE_D), dtype=jnp.float32), 'Wf1': jax.random.normal(ks[3], (FLOW_IN, FLOW_H), dtype=jnp.float32) * (1.0 / np.sqrt(FLOW_IN)), 'bf1': jnp.zeros((FLOW_H,), dtype=jnp.float32), 'Wf2': jax.random.normal(ks[4], (FLOW_H, FLOW_OUT), dtype=jnp.float32) * (1.0 / np.sqrt(FLOW_H)), 'bf2': jnp.zeros((FLOW_OUT,), dtype=jnp.float32), 'Wn1': jax.random.normal(ks[5], (FLOW_OUT, NODE_H), dtype=jnp.float32) * (1.0 / np.sqrt(FLOW_OUT)), 'bn1': jnp.zeros((NODE_H,), dtype=jnp.float32), 'Wn2': jax.random.normal(ks[6], (NODE_H, NODE_OUT), dtype=jnp.float32) * (1.0 / np.sqrt(NODE_H)), 'bn2': jnp.zeros((NODE_OUT,), dtype=jnp.float32)}
    _L0_gnn_all = _L0_gnn_setup()
    _L0_gnn_in = {k: v for k, v in _L0_gnn_all.items() if k in ('Wf1', 'bf1', 'Wf2', 'bf2', 'Wn1', 'bn1', 'Wn2', 'bn2')}
    del _L0_gnn_all

    def _L1_gnn_setup():
        import jax, jax.numpy as jnp
        import numpy as np
        N_NODES = 12500
        N_EDGES = 250000
        D_FEAT = 32
        key = jax.random.key(seed)
        k1, k2 = jax.random.split(key)
        x = jax.random.normal(k1, (N_NODES, D_FEAT), dtype=jnp.float32)
        edge_index = jax.random.randint(k2, (2, N_EDGES), 0, N_NODES, dtype=jnp.int64)
        return {'x': x, 'edge_index': edge_index}
    _L1_gnn_all = _L1_gnn_setup()
    _L1_gnn_in = {k: v for k, v in _L1_gnn_all.items() if k in ()}
    del _L1_gnn_all
    return {'x': x, 'src': src, 'dst': dst, 'edge_attr_16': edge_attr_16, 'L0_gnn_Wf1': _L0_gnn_in['Wf1'], 'L0_gnn_bf1': _L0_gnn_in['bf1'], 'L0_gnn_Wf2': _L0_gnn_in['Wf2'], 'L0_gnn_bf2': _L0_gnn_in['bf2'], 'L0_gnn_Wn1': _L0_gnn_in['Wn1'], 'L0_gnn_bn1': _L0_gnn_in['bn1'], 'L0_gnn_Wn2': _L0_gnn_in['Wn2'], 'L0_gnn_bn2': _L0_gnn_in['bn2']}

def reference(x, src, dst, edge_attr_16, L0_gnn_Wf1, L0_gnn_bf1, L0_gnn_Wf2, L0_gnn_bf2, L0_gnn_Wn1, L0_gnn_bn1, L0_gnn_Wn2, L0_gnn_bn2):
    import jax
    import jax.numpy as jnp

    def _L0_gnn_ref(x, edge_index, edge_attr, Wf1, bf1, Wf2, bf2, Wn1, bn1, Wn2, bn2):
        import jax, jax.numpy as jnp
        import numpy as np
        N_NODES = 6250
        N_EDGES = 100000
        NODE_D, EDGE_D = (32, 16)
        FLOW_IN, FLOW_H, FLOW_OUT = (2 * NODE_D + EDGE_D, 64, 64)
        NODE_H, NODE_OUT = (64, 32)

        def _mlp(h, W1, b1, W2, b2):
            h = jax.nn.relu(h @ W1 + b1)
            return h @ W2 + b2
        past, future = (edge_index[0], edge_index[1])
        x_p = x[past]
        x_f = x[future]
        flow_fwd = jnp.concatenate([x_f, x_p, edge_attr], axis=1)
        flow_bwd = jnp.concatenate([x_p, x_f, edge_attr], axis=1)
        flow_total_in = jnp.concatenate([flow_fwd, flow_bwd], axis=0)
        flow_processed = _mlp(flow_total_in, Wf1, bf1, Wf2, bf2)
        dest = jnp.concatenate([future, past], axis=0)
        flow_total = jax.ops.segment_sum(flow_processed, dest, num_segments=x.shape[0])
        return _mlp(flow_total, Wn1, bn1, Wn2, bn2)

    def _L1_gnn_ref(x, edge_index):
        import jax, jax.numpy as jnp
        import numpy as np
        N_NODES = 12500
        N_EDGES = 250000
        D_FEAT = 32
        row, col = (edge_index[0], edge_index[1])
        messages = x[col]
        out = jax.ops.segment_sum(messages, row, num_segments=x.shape[0])
        return out
    edge_index = jnp.stack([src, dst])
    h = jnp.maximum(_layernorm(x, axis=-1), 0.0)
    x = x + _L0_gnn_ref(h, edge_index, edge_attr_16, L0_gnn_Wf1, L0_gnn_bf1, L0_gnn_Wf2, L0_gnn_bf2, L0_gnn_Wn1, L0_gnn_bn1, L0_gnn_Wn2, L0_gnn_bn2)
    h = jnp.maximum(_layernorm(x, axis=-1), 0.0)
    x = x + _L1_gnn_ref(h, edge_index)
    return x

_drawn_inputs = setup_inputs


def setup_inputs(seed=0):
    import zlib

    import numpy as np

    out = dict(_drawn_inputs(seed))
    spreads = {'L0_gnn_bf1': (0.0, 0.1),
     'L0_gnn_bf2': (0.0, 0.1),
     'L0_gnn_bn1': (0.0, 0.8),
     'L0_gnn_bn2': (0.0, 0.8)}
    factors = {}
    for name, (base, spread) in spreads.items():
        noise = np.random.default_rng([zlib.crc32(name.encode()), seed]).standard_normal(out[name].shape)
        drawn = base * np.exp(spread * noise) if base else spread * noise
        out[name] = jnp.asarray(drawn.astype(out[name].dtype))
    for name, factor in factors.items():
        out[name] = (out[name] * factor).astype(out[name].dtype)
    return out
```

```python
from contextlib import ExitStack

import concourse.bass as bass
from concourse import mybir

P = 128
F32 = mybir.dt.float32
BF16 = mybir.dt.bfloat16
I32 = mybir.dt.int32
U32 = mybir.dt.uint32
ALU = mybir.AluOpType
ACT = mybir.ActivationFunctionType
AX = mybir.AxisListType.X

N, D, E, EA, HID = 12500, 32, 200000, 16, 64
NB = -(-N // P)
U = 4
R = 4
NBP = -(-(NB + 1) // U) * U
NI = -(-(-(-E // P) + NB) // (U * R))
J = NI * U * R
NP, NC = 125, E // 125
REC = HID + 3
ACC = HID + 1
FAR = 32768
BIG = float(1 << 22)
JC = J // 4
assert E % 125 == 0 and JC <= 512 and J % 4 == 0 and NBP % 4 == 0


class Chain:

    def __init__(self, eng, sem, tick=None):
        self.eng, self.sem, self.n, self.base, self.tick = eng, sem, 0, 0, tick

    def link(self, ins):
        self.n += 1
        ins.then_inc(self.sem, 1)
        return self.n

    def wait(self, mark=None):
        self.eng.wait_ge(self.sem, self.base + (self.n if mark is None else mark))
        if self.tick is not None:
            self.eng.sem_inc(self.tick, 1)

    def step(self, ins):
        self.link(ins)
        self.wait()


def bcast(ap, n):
    return ap.unsqueeze(2).broadcast_to([ap.shape[0], ap.shape[1], n])


def bcast_mid(ap, n):
    return ap.unsqueeze(1).broadcast_to([ap.shape[0], n, ap.shape[1]])


def build(nc, x, sd, ea, Wf1, bf1, Wf2, bf2, Wn1, bn1, Wn2, bn2, out):
    with ExitStack() as ctx:
        def sb(name, shape, dt=F32):
            return ctx.enter_context(nc.sbuf_tensor(name, shape, dt))

        def sem(name):
            return ctx.enter_context(nc.semaphore(name))

        def sems(name, n):
            return [sem(f"{name}{i}") for i in range(n)]

        def dram(name, shape, dt=F32):
            return nc.dram_tensor(name, shape, dt).ap()

        by_d_sd = dram("by_d_sd", [E + P, 2], I32)
        by_d_ea = dram("by_d_ea", [E + P, EA])
        t2_rows = dram("t2_rows", [NBP * P, P])
        records = dram("records", [E + P, REC])
        h2_rows = dram("h2_rows", [NBP * P, D])

        iota128 = sb("iota128", [P, P])
        iota_blk1 = sb("iota_blk1", [P, NB])
        thr = sb("thr", [P, NB])
        thr_half = sb("thr_half", [P, NB])
        ones = sb("ones", [P, P])
        ident = sb("ident", [P, P])
        before = sb("before", [P, P])
        upto = sb("upto", [P, P])
        ones_h = sb("ones_h", [P, P], BF16)
        before_h = sb("before_h", [P, P], BF16)
        tail_sd = sb("tail_sd", [P, 2], I32)
        tail_rec = sb("tail_rec", [P, REC])
        w12 = sb("w12", [P, 2 * P])
        b1b1 = sb("b1b1", [P, P])
        wee = sb("wee", [EA, P])
        wf2e = sb("wf2e", [ACC, HID])
        wn1 = sb("wn1", [HID, HID])
        bn1c = sb("bn1c", [HID, 1])
        wn2 = sb("wn2", [HID, D])
        bn2r = sb("bn2r", [1, D])
        xs = sb("xs", [P, NBP, D])
        h = sb("h", [P, NBP, D])
        lnt = sb("lnt", [P, NBP, D])
        stat = sb("stat", [P, 2, NBP])
        t1 = sb("t1", [P, NBP, P])
        acc = sb("acc", [P, NBP, ACC])
        acc_flat = acc[:, :, :].rearrange("p b c -> p (b c)")
        jrow = acc_flat[0:NB, 0:J]
        ge = acc_flat[0:NB, J:2 * J]
        dblkf = acc_flat[0:NP, 2 * J:2 * J + NC]
        assert 2 * J + NC <= NBP * ACC
        acc2 = t1[:, 0:NBP // U, :].rearrange("p b (u f) -> p (b u) f", f=D)
        hs = sb("hs", [P, P])
        hT = sb("hT", [P, P])
        t2s = sb("t2s", [P, U, P])
        raw = sb("raw", [P, 2, J], I32)
        nat = raw[:, :, :].rearrange("p k j -> p (k j)")[0:NP, 0:2 * NC].rearrange("p (c k) -> p c k", k=2)
        dcol = raw[:, 0, :]
        sloc = raw[:, 1, :].bitcast(F32)
        wide = sb("wide", [P, 2, J])
        natf = wide[0:NP, :, 0:NC]
        base_row = [wide[:, k, :] for k in range(2)]
        dblk = lnt[0:NP, 0:NC // D, :].rearrange("p b f -> p (b f)").bitcast(I32)
        assert NC % D == 0
        e0f = lnt[0:1, 0:J // D, :].rearrange("p b f -> p (b f)")
        junk_a = sb("junk_a", [NP, NC], BF16)
        junk_d = sb("junk_d", [NP, NC], BF16)
        row_next = sb("row_next", [NP, 2], I32)
        row_nextf = sb("row_nextf", [NP, 1])
        viol = sb("viol", [NP, 3])
        flag = sb("flag", [1, 1], I32)
        cum = sb("cum", [NP, 2, NB + 1])
        cnt = sb("cnt", [NP, 2, NB])
        ssum = sb("ssum", [NP, NB])
        ncol = sb("ncol", [NB, 2])
        tcol_i = sb("tcol_i", [NB, 2], I32)
        tcol = sb("tcol", [NB, 2])
        tend = sb("tend", [NB, 2])
        slack = sb("slack", [NB, 2])
        c128 = sb("c128", [NB, P])
        sched = sb("sched", [P, J], I32)
        e0 = [sched[32 * k:32 * k + 1, :] for k in (0, 1)]
        blk = [sched[32 * k:32 * k + 1, :] for k in (2, 3)]
        rec = sb("rec", [P, R, U, REC])
        rec_i = sb("rec_i", [P, R, U, 2], I32)
        eat = sb("eat", [P, R, U, EA])
        g2 = sb("g2", [P, R, U, P])
        sdf = sb("sdf", [P, 2, U, 2])
        small = sb("small", [P, 2, 7, U])
        sblk = sb("sblk", [P, 2, U], I32)
        ohd = sb("ohd", [P, 2, U, P])
        ohs = sb("ohs", [P, 2, U, NB], BF16)
        prod = sb("prod", [P, U, NB])
        pos = sb("pos", [P, R, U], I32)
        q_row = sb("q_row", [P, 2, NB])
        oht = sb("oht", [P, 2, U, P])
        eaT = sb("eaT", [EA, 2, U, P])
        rf = sb("rf", [P, U, ACC])
        srec = rec
        ssrc = sb("ssrc", [P, 2, U])
        didx = sb("didx", [P, R, U], I32)
        h2g = sb("h2g", [P, R, U, D])
        accs = sb("accs", [P, U, ACC])
        accT = sb("accT", [ACC, U * P])
        flowT = sb("flowT", [HID, U * P])
        nodeT = sb("nodeT", [HID, U * P])
        bn2b = sb("bn2b", [P, D])

        fb_base = sb("fb_base", [NP, NB])[:, :]
        fb_blk = sb("fb_blk", [NP, 1])
        fb_oh = sb("fb_oh", [NP, NB])
        fb_prod = sb("fb_prod", [NP, P])
        fb_pos = sb("fb_pos", [NP, 1])
        fb_posi = sb("fb_posi", [NP, 1], I32)
        fb_sd = sb("fb_sd", [NP, 2], I32)
        fb_ea = sb("fb_ea", [NP, EA])
        fb_own = sem("fb_own")

        pb = [ctx.enter_context(nc.psum_tensor(f"bank{i}", [P, 512], F32)) for i in range(8)]
        tab = [pb[1], pb[2], pb[3], pb[5]]

        x_in, w_in, nat_in = sem("x_in"), sem("w_in"), sem("nat_in")
        by_d_copied = sem("by_d_copied")
        tails_set = sem("tails_set")
        consts = sem("consts")
        pool_own, dve_own, act_own = sem("pool_own"), sem("dve_own"), sem("act_own")
        rearranged = sem("rearranged")
        var_ready, std_ready, h_ready = sem("var_ready"), sem("std_ready"), sem("h_ready")
        hs_ready, hsT_ready, hT_ready, tab_ready = sem("hs_ready"), sem("hsT_ready"), sem("hT_ready"), sem("tab_ready")
        t1_ready, t2s_ready, t2_written = sem("t1_ready"), sem("t2s_ready"), sem("t2_written")
        b1_ready = sem("b1_ready")
        nat_ready = sem("nat_ready")
        s_cum = sem("s_cum")
        d_cum = sem("d_cum")
        cnt_ready, n_ready, tiles_ready, tend_ready = sem("cnt_ready"), sem("n_ready"), sem("tiles_ready"), sem("tend_ready")
        ge_ready, sched_ps, sched_read, sched_done = sem("ge_ready"), sem("sched_ps"), sem("sched_read"), sem("sched_done")
        viol_ready, flag_ps, flag_ready = sem("viol_ready"), sem("flag_ps"), sem("flag_ready")
        begin_ps = sem("begin_ps")
        fbase_ps, fbase_ready = sem("fbase_ps"), sem("fbase_ready")
        fb_ld, fb_sc = sem("fb_ld"), sems("fb_sc", 2)
        ld_sd, ld_ea, gat, sct = sems("ld_sd", R), sems("ld_ea", R), sems("gat", R), sems("sct", R)
        ohd_ready, ohs_ready, tp_ready, oht_ready = sem("ohd_ready"), sem("ohs_ready"), sem("tp_ready"), sem("oht_ready")
        q_ready, q_read, pos_ready = sem("q_ready"), sem("q_read"), sem("pos_ready")
        pre_ready, relu_ready, sum_ready, acc_done = sem("pre_ready"), sem("relu_ready"), sem("sum_ready"), sem("acc_done")
        pool_tick, act_tick, pe_tick, dve_tick = sem("pool_tick"), sem("act_tick"), sem("pe_tick"), sem("dve_tick")
        dve_d = sem("dve_d")
        ld_srec = sems("ld_srec", R)
        soh_ready, ssum_ready, sacc_done, dve_s = sem("soh_ready"), sem("ssum_ready"), sem("sacc_done"), sem("dve_s")
        accs_ready, accT_ps, accT_ready = sem("accs_ready"), sem("accT_ps"), sem("accT_ready")
        flow_ps, flow_ready, node_ps, node_ready = sem("flow_ps"), sem("flow_ready"), sem("node_ps"), sem("node_ready")
        outp_ps, x1_done, dve_n = sem("outp_ps"), sem("x1_done"), sem("dve_n")
        var2_ready, std2_ready, h2_ready, h2_written = sem("var2_ready"), sem("std2_ready"), sem("h2_ready"), sem("h2_written")
        didx_ready, gh = sem("didx_ready"), sems("gh", R)
        noh_ready, nsum_ready, nacc_done, dve_g = sem("noh_ready"), sem("nsum_ready"), sem("nacc_done"), sem("dve_g")
        acc2_zero, y_ready, y_out = sem("acc2_zero"), sem("y_ready"), sem("y_out")

        block = ctx.enter_context(nc.Block())
        N_FULL = N // P
        N_TAIL = N - N_FULL * P

        def four(eng, row, j0, top):
            return nc.values_load_multi_w_load_instructions(
                row[0:1, bass.ds(j0, U)], engines=[eng.engine], min_val=0, max_val=top,
                skip_runtime_bounds_check_because="the schedule clamps it to this range")[1]

        def rounds(eng, body):
            body(0, True, False)
            with eng.Fori(1, NI - 1) as i:
                body(i, False, False)
            body(NI - 1, False, True)

        @block.sync
        def _(sp):
            sp.dma_start(nat[:, :, :], sd.rearrange("(p c) k -> p c k", p=NP)).then_inc(nat_in, 16)
            sp.dma_start(row_next[0:NP - 1, :], sd.rearrange("(p c) k -> p c k", p=NP)[1:NP, 0, :]).then_inc(nat_in, 16)
            sp.dma_start(xs[:, 0:N_FULL, :], x[0:N_FULL * P, :].rearrange("(b p) f -> p b f", p=P)).then_inc(x_in, 16)
            sp.wait_ge(tails_set, 1)
            sp.dma_start(xs[0:N_TAIL, N_FULL, :], x[N_FULL * P:N, :]).then_inc(x_in, 16)
            n_w = 0
            for u in range(4):
                for c, r0 in enumerate((0, D, D, 0)):
                    sp.dma_start(w12[u * D:(u + 1) * D, c * HID:(c + 1) * HID], Wf1[r0:r0 + D, :]).then_inc(w_in, 16)
                    n_w += 1
            for c in range(2):
                for u in range(4):
                    sp.dma_start(b1b1[u * D:u * D + 1, c * HID:(c + 1) * HID], bf1.unsqueeze(0)).then_inc(w_in, 16)
                    n_w += 1
                sp.dma_start(wee[:, c * HID:(c + 1) * HID], Wf1[2 * D:2 * D + EA, :]).then_inc(w_in, 16)
                n_w += 1
            for dst_, src_ in ((wf2e[0:HID, :], Wf2), (wf2e[HID:ACC, :], bf2.unsqueeze(0)), (wn1[:, :], Wn1),
                               (bn1c[:, :], bn1.unsqueeze(1)), (wn2[:, :], Wn2), (bn2r[:, :], bn2.unsqueeze(0))):
                sp.dma_start(dst_, src_).then_inc(w_in, 16)
                n_w += 1
            assert n_w == N_W
            for to, of in ((by_d_sd, sd), (by_d_ea, ea)):
                sp.dma_start(to[0:E, :].rearrange("(p c) f -> p (c f)", p=1600),
                             of.rearrange("(p c) f -> p (c f)", p=1600)).then_inc(by_d_copied, 16)
            sp.dma_start(by_d_sd[E:E + P, :], tail_sd[:, :]).then_inc(by_d_copied, 16)
            sp.dma_start(by_d_ea[E:E + P, :], tail_rec[:, 0:EA]).then_inc(by_d_copied, 16)
            sp.dma_start(records[E:E + P, :], tail_rec[:, :]).then_inc(by_d_copied, 16)

            def store_t2(i):
                sp.wait_ge(t2s_ready, i + 1)
                sp.dma_start(t2_rows[bass.ds(i * (U * P), U * P), :].rearrange("(u p) f -> p u f", p=P),
                             t2s[:, :, :]).then_inc(t2_written, 16)
            store_t2(0)
            with sp.Fori(1, NBP // U) as i:
                store_t2(i)

            sp.wait_ge(sched_done, 2)
            sp.wait_ge(rearranged, 1)

            def load_edges(i, first, last):
                for r in range(R):
                    at = four(sp, e0[1], i * (U * R) + r * U, E)
                    if not first:
                        sp.wait_ge(relu_ready, i * R + r + 1 - R)
                    for u in range(U):
                        sp.dma_start(rec_i[:, r, u, :], by_d_sd[bass.ds(at[u], P), :]).then_inc(ld_sd[r], 16)
                    for u in range(U):
                        sp.dma_start(eat[:, r, u, :], by_d_ea[bass.ds(at[u], P), :]).then_inc(ld_ea[r], 16)
            rounds(sp, load_edges)

            for r in range(R):
                sp.wait_ge(sct[r], 16 * U * NI)

            def load_records(i, first, last):
                for r in range(R):
                    at = four(sp, e0[0], i * (U * R) + r * U, E)
                    if not first:
                        sp.wait_ge(ssum_ready, i * R + r + 1 - R)
                    for u in range(U):
                        sp.dma_start(srec[:, r, u, :], records[bass.ds(at[u], P), :]).then_inc(ld_srec[r], 16)
            rounds(sp, load_records)

            sp.wait_ge(h2_ready, 1)
            sp.dma_start(h2_rows.rearrange("(b p) f -> p b f", p=P), h[:, :, :]).then_inc(h2_written, 16)
            sp.wait_ge(y_ready, 1)
            sp.dma_start(out[0:N_FULL * P, :].rearrange("(b p) f -> p b f", p=P), lnt[:, 0:N_FULL, :]).then_inc(y_out, 16)
            sp.dma_start(out[N_FULL * P:N, :], lnt[0:N_TAIL, N_FULL, :]).then_inc(y_out, 16)
            sp.wait_ge(y_out, 32)
            sp.wait_ge(h2_written, 16)
            sp.wait_ge(by_d_copied, 80)
            sp.wait_ge(t2_written, 16 * (NBP // U))

        FB_STEPS = 13

        def rearrange_edges(pool):
            ea_cols = ea.rearrange("(p c) f -> p c f", p=NP)
            last_row = pool.to_reg(E - 1)

            def column(c):
                own = Chain(pool, fb_own, pool_tick)
                own.base = c * FB_STEPS
                pool.dma_start(fb_ea[:, :], ea_cols[:, bass.ds(c, 1), :].rearrange("p a f -> p (a f)")).then_inc(fb_ld, 16)
                own.link(nc.gpsimd.tensor_copy(fb_blk[:, :], dblkf[:, bass.ds(c, 1)]))
                own.link(nc.gpsimd.tensor_copy(fb_sd[:, :], nat[:, bass.ds(c, 1), :].rearrange("p a k -> p (a k)")))
                own.wait()
                own.step(nc.gpsimd.tensor_scalar(fb_oh[:, :], iota128[0:NP, 0:NB], fb_blk[:, 0:1], None, ALU.is_equal))
                own.step(nc.gpsimd.tensor_tensor(fb_prod[:, 0:NB], fb_oh[:, :], fb_base, ALU.mult))
                for w in (64, 32, 16, 8, 4, 2):
                    own.step(nc.gpsimd.tensor_tensor(fb_prod[:, 0:w], fb_prod[:, 0:w], fb_prod[:, w:2 * w], ALU.add))
                own.link(nc.gpsimd.tensor_tensor(fb_pos[:, :], fb_prod[:, 0:1], fb_prod[:, 1:2], ALU.add))
                own.step(nc.gpsimd.tensor_tensor(fb_base, fb_base, fb_oh[:, :], ALU.add))
                own.link(nc.gpsimd.tensor_copy(fb_posi[:, :], fb_pos[:, :]))
                own.wait()
                assert own.n == FB_STEPS
                pool.wait_ge(fb_ld, 16 * (c + 1))
                pool.sem_inc(pool_tick, 1)
                for k, (rows, to) in enumerate(((fb_sd, by_d_sd), (fb_ea, by_d_ea))):
                    nc.gpsimd.indirect_dma_start(
                        out=to, out_offset=bass.IndirectOffsetOnAxis(ap=fb_posi[:, :].bitcast(U32), axis=0),
                        in_=rows[:, :], in_offset=None, bounds_check=last_row, oob_is_err=False).then_inc(fb_sc[k], 16)
                for k in range(2):
                    pool.wait_ge(fb_sc[k], 16 * (c + 1))
                    pool.sem_inc(pool_tick, 1)
            with pool.Fori(0, NC) as c:
                column(c)

        @block.gpsimd
        def _(pool):
            nc.gpsimd.memset(xs[:, N_FULL:NBP, :], 0.0)
            nc.gpsimd.memset(tail_rec[:, 0:HID + 1], 0.0)
            nc.gpsimd.memset(fb_prod[:, :], 0.0)
            nc.gpsimd.memset(tail_sd[:, 0:1], 0)
            nc.gpsimd.memset(tail_sd[:, 1:2], FAR)
            nc.gpsimd.memset(tail_rec[:, HID + 1:HID + 2].bitcast(I32), FAR)
            nc.gpsimd.memset(tail_rec[:, HID + 2:HID + 3].bitcast(I32), 0).then_inc(tails_set, 1)
            own = Chain(pool, pool_own)
            nc.gpsimd.iota(iota128[:, :], [[1, P]], base=0, channel_multiplier=0, allow_small_or_imprecise_dtypes=True)
            nc.gpsimd.iota(iota_blk1[:, :], [[1, NB]], base=1, channel_multiplier=0, allow_small_or_imprecise_dtypes=True)
            nc.gpsimd.iota(jrow[:, :], [[1, J]], base=0, channel_multiplier=0, allow_small_or_imprecise_dtypes=True)
            nc.gpsimd.memset(ones[:, :], 1.0)
            nc.gpsimd.memset(ones_h[:, :], 1.0)
            nc.gpsimd.memset(c128[:, :], float(P))
            nc.gpsimd.memset(cum[:, :, 0:1], 0.0)
            nc.gpsimd.memset(rf[:, :, HID:ACC], 1.0)
            nc.gpsimd.memset(rec[:, :, :, HID:HID + 1], 1.0)
            own.step(nc.gpsimd.iota(thr[:, :], [[P, NB]], base=P, channel_multiplier=0, allow_small_or_imprecise_dtypes=True))
            nc.gpsimd.tensor_scalar(thr_half[:, :], thr[:, :], -0.5, None, ALU.add)
            for m, op in ((before, ALU.is_gt), (upto, ALU.is_ge), (ident, ALU.is_equal), (before_h, ALU.is_gt)):
                ins = nc.gpsimd.affine_select(out=m[:, :], in_=ones[:, :], compare_op=op, fill=0.0, base=0,
                                              pattern=[[1, P]], channel_multiplier=-1)
            ins.then_inc(consts, 1)

            pool.wait_ge(by_d_copied, 80)
            pool.wait_ge(flag_ready, 1)
            pool.wait_ge(fbase_ready, 1)
            unsorted_edges = pool.value_load(flag[0:1, 0:1], min_val=0, max_val=1 << 20)
            with pool.If(unsorted_edges > 0):
                rearrange_edges(pool)
            with pool.Else():
                pool.sem_inc(pool_tick, 1)
            pool.sem_inc(rearranged, 1)

            pool.wait_ge(t2_written, 16 * (NBP // U))
            end = pool.to_reg(E - 1)

            def gather_t2(i, r):
                pool.wait_ge(ld_sd[r], 16 * U * (i + 1))
                pool.sem_inc(pool_tick, 1)
                for u in range(U):
                    nc.gpsimd.indirect_dma_start(
                        out=g2[:, r, u, :], out_offset=None, in_=t2_rows,
                        in_offset=bass.IndirectOffsetOnAxis(ap=rec_i[:, r, u, 0:1].bitcast(U32), axis=0)).then_inc(gat[r], 16)

            def scatter_records(i, r):
                pool.wait_ge(pos_ready, i * R + r + 1)
                pool.sem_inc(pool_tick, 1)
                pool.wait_ge(relu_ready, i * R + r + 1)
                pool.sem_inc(pool_tick, 1)
                for u in range(U):
                    nc.gpsimd.indirect_dma_start(
                        out=records, out_offset=bass.IndirectOffsetOnAxis(ap=pos[:, r, u:u + 1].bitcast(U32), axis=0),
                        in_=rec[:, r, u, :], in_offset=None, bounds_check=end, oob_is_err=False).then_inc(sct[r], 16)

            def edges(i, first, last):
                for r in range(R):
                    if r < R - 2:
                        gather_t2(i, r + 2)
                    elif not last:
                        gather_t2(i + 1, r + 2 - R)
                    scatter_records(i, r)
            gather_t2(0, 0)
            gather_t2(0, 1)
            rounds(pool, edges)

            pool.wait_ge(pre_ready, NI * R)
            nc.gpsimd.memset(acc2[:, :, :], 0.0).then_inc(acc2_zero, 1)
            pool.wait_ge(h2_written, 16)

            def gather_h2(i, first, last):
                for r in range(R):
                    pool.wait_ge(didx_ready, i * R + r + 1)
                    pool.sem_inc(pool_tick, 1)
                    if not first:
                        pool.wait_ge(nsum_ready, i * R + r + 1 - R)
                        pool.sem_inc(pool_tick, 1)
                    for u in range(U):
                        nc.gpsimd.indirect_dma_start(
                            out=h2g[:, r, u, :], out_offset=None, in_=h2_rows,
                            in_offset=bass.IndirectOffsetOnAxis(ap=didx[:, r, u:u + 1].bitcast(U32), axis=0)).then_inc(gh[r], 16)
            rounds(pool, gather_h2)

        @block.scalar
        def _(act):
            act.wait_ge(var_ready, 1)
            nc.scalar.activation(stat[:, 1, :], stat[:, 1, :], ACT.Sqrt).then_inc(std_ready, 1)
            act.wait_ge(h_ready, 1)

            def tables(i, first):
                if not first:
                    act.wait_ge(hsT_ready, i)
                    act.sem_inc(act_tick, 1)
                nc.scalar.activation(hs[:, :].rearrange("p (u f) -> p u f", u=U), h[:, bass.ds(i * U, U), :], ACT.Copy).then_inc(hs_ready, 1)
                act.wait_ge(hsT_ready, i + 1)
                nc.scalar.activation(hT[:, :], pb[0][:, 0:P], ACT.Copy).then_inc(hT_ready, 1)
                act.wait_ge(tab_ready, i + 1)
                act.sem_inc(act_tick, 1)
                for u in range(U):
                    ins = nc.scalar.activation(t1[:, bass.ds(i * U + u, 1), :].rearrange("p a c -> p (a c)"), tab[u][:, 0:P], ACT.Copy)
                ins.then_inc(t1_ready, 1)
                if not first:
                    act.wait_ge(t2_written, 16 * i)
                    act.sem_inc(act_tick, 1)
                for u in range(U):
                    ins = nc.scalar.activation(t2s[:, u, :], tab[u][:, P:2 * P], ACT.Copy)
                ins.then_inc(t2s_ready, 1)
            tables(0, True)
            with act.Fori(1, NBP // U) as i:
                tables(i, False)

            act.wait_ge(nat_ready, 1)
            act.wait_ge(consts, 1)
            def count_src(b, first):
                if not first:
                    act.wait_ge(s_cum, b)
                    act.sem_inc(act_tick, 1)
                nc.scalar.activation(junk_a[:, :], natf[:, 0, :], ACT.Sign, bias=thr_half[0:NP, bass.ds(b, 1)], scale=-1.0,
                                     accum_out=ssum[:, bass.ds(b, 1)]).then_inc(s_cum, 1)
            count_src(0, True)
            with act.Fori(1, NB) as b:
                count_src(b, False)

            def transposed(i, r):
                v = i * R + r + 1
                act.wait_ge(tp_ready, v)
                nc.scalar.activation(oht[:, r % 2, :, :].rearrange("p u n -> p (u n)"), pb[0][:, :], ACT.Copy)
                nc.scalar.activation(eaT[:, r % 2, :, :].rearrange("p u n -> p (u n)"), pb[1][0:EA, :], ACT.Copy).then_inc(oht_ready, 1)

            def hidden(i, r, first):
                v = i * R + r + 1
                act.wait_ge(pre_ready, v)
                pre = pb[2][:, :].rearrange("p (u c) -> p u c", u=U)
                if not (first and r == 0):
                    act.wait_ge(sum_ready, v - 1)
                nc.scalar.activation(rf[:, :, 0:HID], pre[:, :, 0:HID], ACT.Relu)
                if not first:
                    act.wait_ge(sct[r], 16 * U * i)
                    act.sem_inc(act_tick, 1)
                nc.scalar.copy(rec[:, r, :, HID + 1:REC].bitcast(I32), rec_i[:, r, :, :])
                nc.scalar.activation(rec[:, r, :, 0:HID], pre[:, :, HID:P], ACT.Relu).then_inc(relu_ready, 1)

            def edges(i, first, last):
                for r in range(R):
                    hidden(i, r, first)
                    if r < R - 1:
                        transposed(i, r + 1)
                    elif not last:
                        transposed(i + 1, 0)
            transposed(0, 0)
            rounds(act, edges)

            def nodes(i, first):
                if not first:
                    act.wait_ge(accT_ps, i)
                    act.sem_inc(act_tick, 1)
                nc.scalar.activation(accs[:, :, :], acc[:, bass.ds(i * U, U), :], ACT.Copy).then_inc(accs_ready, 1)
                act.wait_ge(accT_ps, i + 1)
                nc.scalar.activation(accT[:, :], pb[0][0:ACC, :], ACT.Copy).then_inc(accT_ready, 1)
                act.wait_ge(flow_ps, i + 1)
                nc.scalar.activation(flowT[:, :], pb[1][0:HID, :], ACT.Copy).then_inc(flow_ready, 1)
                act.wait_ge(node_ps, i + 1)
                nc.scalar.activation(nodeT[:, :], pb[2][0:HID, :], ACT.Relu, bias=bn1c[:, :]).then_inc(node_ready, 1)
            act.wait_ge(sacc_done, NI * R)
            nodes(0, True)
            with act.Fori(1, NBP // U) as i:
                nodes(i, False)
            act.wait_ge(var2_ready, 1)
            nc.scalar.activation(stat[:, 1, :], stat[:, 1, :], ACT.Sqrt).then_inc(std2_ready, 1)

            def indices(i, first, last):
                for r in range(R):
                    if not first:
                        act.wait_ge(gh[r], 16 * U * i)
                        act.sem_inc(act_tick, 1)
                    nc.scalar.copy(didx[:, r, :], dcol[:, bass.ds(i * (U * R) + r * U, U)]).then_inc(didx_ready, 1)
            rounds(act, indices)

        @block.tensor
        def _(pe):
            pe.wait_ge(consts, 1)
            pe.wait_ge(w_in, 16 * N_W)

            def tables(i, first):
                pe.wait_ge(hs_ready, i + 1)
                nc.tensor.transpose(pb[0][:, 0:P], hs[:, :], ident[:, :]).then_inc(hsT_ready, 1)
                if not first:
                    pe.wait_ge(t2s_ready, i)
                    pe.sem_inc(pe_tick, 1)
                pe.wait_ge(hT_ready, i + 1)
                for u in range(U):
                    o = tab[u][:, 0:2 * P]
                    nc.tensor.matmul(o, hT[u * D:(u + 1) * D, :], w12[u * D:(u + 1) * D, :], start=True, stop=False)
                    ins = nc.tensor.matmul(o[:, P:2 * P], ones[u * D:u * D + 1, :], b1b1[u * D:u * D + 1, :], start=False, stop=True)
                ins.then_inc(tab_ready, 1)
            tables(0, True)
            with pe.Fori(1, NBP // U) as i:
                tables(i, False)

            pe.wait_ge(t2s_ready, NBP // U)
            for n, k in enumerate((1, 0)):
                pe.wait_ge(cnt_ready, n + 1)
                nc.tensor.matmul(pb[3][0:NB, 0:1], cnt[:, k, :], ones[0:NP, 0:1], start=True, stop=True).then_inc(n_ready, 1)
                pe.wait_ge(tiles_ready, n + 1)
                nc.tensor.matmul(pb[3][0:NB, 1:2], upto[0:NB, 0:NB], tcol[:, k:k + 1], start=True, stop=True).then_inc(tend_ready, 1)
                pe.wait_ge(ge_ready, n + 1)
                for c in range(J // JC):
                    w = n * (J // JC) + c
                    if w:
                        pe.wait_ge(sched_read, w)
                    cols = ge[:, c * JC:(c + 1) * JC]
                    nc.tensor.matmul(pb[4][:, 0:JC], c128[:, :], cols, start=True, stop=True)
                    nc.tensor.matmul(pb[5][0:1, 0:JC], slack[:, k:k + 1], cols, start=True, stop=True)
                    nc.tensor.matmul(pb[6][0:1, 0:JC], ones[0:NB, 0:1], cols, start=True, stop=True).then_inc(sched_ps, 1)
                if k == 1:
                    nc.tensor.matmul(pb[7][0:NP, 0:NB], ones[0:NP, 0:NP], cum[:, 1, 0:NB], start=True, stop=False)
                    nc.tensor.matmul(pb[7][0:NP, 0:NB], before[0:NP, 0:NP], cnt[:, 1, :], start=False, stop=True).then_inc(fbase_ps, 1)
                    pe.wait_ge(viol_ready, 1)
                    pe.wait_ge(fbase_ready, 1)
                    nc.tensor.matmul(pb[7][0:1, 256:257], viol[:, 2:3], ones[0:NP, 0:1], start=True, stop=True).then_inc(flag_ps, 1)

            pe.wait_ge(flag_ready, 1)
            nc.tensor.matmul(pb[7][:, 0:NB], ones[0:NP, :], cum[:, 0, 0:NB], start=True, stop=True).then_inc(begin_ps, 1)
            q = pb[4][:, 0:(U + 1) * NB].rearrange("p (u b) -> p u b", b=NB)

            def transposes(i, r, very_first=False):
                v = i * R + r + 1
                if not very_first:
                    pe.wait_ge(oht_ready, v - 1)
                    pe.sem_inc(pe_tick, 1)
                pe.wait_ge(ohd_ready, v)
                for u in range(U):
                    nc.tensor.transpose(pb[0][:, u * P:(u + 1) * P], ohd[:, r % 2, u, :], ident[:, :])
                pe.wait_ge(ld_ea[r], 16 * U * (i + 1))
                for u in range(U):
                    ins = nc.tensor.transpose(pb[1][0:EA, u * P:(u + 1) * P], eat[:, r, u, :], ident[:, :])
                ins.then_inc(tp_ready, 1)

            def hidden(i, r):
                v = i * R + r + 1
                at = four(pe, blk[1], i * (U * R) + r * U, NB)
                pe.wait_ge(gat[r], 16 * U * (i + 1))
                pe.sem_inc(pe_tick, 1)
                pe.wait_ge(oht_ready, v)
                for u in range(U):
                    p = pb[2][:, u * P:(u + 1) * P]
                    nc.tensor.matmul(p, ident[:, :], g2[:, r, u, :], start=True, stop=False)
                    nc.tensor.matmul(p, eaT[:, r % 2, u, :], wee[:, :], start=False, stop=False)
                    ins = nc.tensor.matmul(p, oht[:, r % 2, u, :], t1[:, bass.ds(at[u], 1), :].rearrange("p a c -> p (a c)"), start=False, stop=True)
                ins.then_inc(pre_ready, 1)

            def counts(i, r, first):
                v = i * R + r + 1
                o = ohs[:, r % 2, :, :]
                if not (first and r == 0):
                    pe.wait_ge(q_read, v - 1)
                    pe.sem_inc(pe_tick, 1)
                pe.wait_ge(ohs_ready, v)
                nc.tensor.matmul(q[:, 0:U, :], before_h[:, :], o, start=True, stop=False)
                nc.tensor.matmul(q[:, U, :], ones_h[:, :], o[:, 0, :], start=False, stop=False)
                nc.tensor.matmul(q[:, 1:U, :], ones_h[:, :], bcast_mid(o[:, 0, :], U - 1), start=False, stop=False)
                for c in range(1, U):
                    ins = nc.tensor.matmul(q[:, c + 1:U + 1, :], ones_h[:, :], bcast_mid(o[:, c, :], U - c), start=False, stop=c == U - 1)
                ins.then_inc(q_ready, 1)

            def sums(i, r, first):
                v = i * R + r + 1
                if not (first and r == 0):
                    pe.wait_ge(acc_done, v - 1)
                    pe.sem_inc(pe_tick, 1)
                pe.wait_ge(relu_ready, v)
                for u in range(U):
                    ins = nc.tensor.matmul(pb[3][:, u * ACC:(u + 1) * ACC], ohd[:, r % 2, u, :], rf[:, u, :], start=True, stop=True)
                ins.then_inc(sum_ready, 1)

            def edges(i, first, last):
                for r in range(R):
                    hidden(i, r)
                    if r < R - 1:
                        transposes(i, r + 1)
                    elif not last:
                        transposes(i + 1, 0)
                    counts(i, r, first)
                    sums(i, r, first)
            transposes(0, 0, True)
            rounds(pe, edges)

            def sum_records(i, first, last):
                for r in range(R):
                    v = i * R + r + 1
                    if not (first and r < 2):
                        pe.wait_ge(sacc_done, v - 2)
                        pe.sem_inc(pe_tick, 1)
                    pe.wait_ge(soh_ready, v)
                    for u in range(U):
                        ins = nc.tensor.matmul(pb[5 + r % 2][:, u * ACC:(u + 1) * ACC], ohd[:, r % 2, u, :],
                                               srec[:, r, u, 0:ACC], start=True, stop=True)
                    ins.then_inc(ssum_ready, 1)
            rounds(pe, sum_records)

            nc.tensor.matmul(pb[7][:, 0:D], ones[0:1, :], bn2r[:, :], start=True, stop=True).then_inc(b1_ready, 1)

            def nodes(i, first):
                pe.wait_ge(accs_ready, i + 1)
                for u in range(U):
                    ins = nc.tensor.transpose(pb[0][0:ACC, u * P:(u + 1) * P], accs[:, u, :], ident[:, :])
                ins.then_inc(accT_ps, 1)
                pe.wait_ge(accT_ready, i + 1)
                nc.tensor.matmul(pb[1][0:HID, :], wf2e[:, :], accT[:, :], start=True, stop=True).then_inc(flow_ps, 1)
                pe.wait_ge(flow_ready, i + 1)
                pe.sem_inc(pe_tick, 1)
                nc.tensor.matmul(pb[2][0:HID, :], wn1[:, :], flowT[:, :], start=True, stop=True).then_inc(node_ps, 1)
                if not first:
                    pe.wait_ge(x1_done, i)
                    pe.sem_inc(pe_tick, 1)
                pe.wait_ge(node_ready, i + 1)
                for u in range(U):
                    ins = nc.tensor.matmul(pb[3][:, u * D:(u + 1) * D], nodeT[:, u * P:(u + 1) * P], wn2[:, :], start=True, stop=True)
                ins.then_inc(outp_ps, 1)
            nodes(0, True)
            with pe.Fori(1, NBP // U) as i:
                nodes(i, False)

            def sum_neighbours(i, first, last):
                for r in range(R):
                    v = i * R + r + 1
                    if not (first and r < 2):
                        pe.wait_ge(nacc_done, v - 2)
                        pe.sem_inc(pe_tick, 1)
                    pe.wait_ge(gh[r], 16 * U * (i + 1))
                    pe.sem_inc(pe_tick, 1)
                    pe.wait_ge(noh_ready, v)
                    for u in range(U):
                        ins = nc.tensor.matmul(pb[5 + r % 2][:, u * D:(u + 1) * D], ohd[:, r % 2, u, :], h2g[:, r, u, :],
                                               start=True, stop=True)
                    ins.then_inc(nsum_ready, 1)
            rounds(pe, sum_neighbours)

        @block.vector
        def _(dve):
            own = Chain(dve, dve_own)

            def norm_relu(src, var_sem, std_sem):
                own.step(nc.vector.reduce_sum(stat[:, 0, :], src[:, :, :], axis=AX))
                own.step(nc.vector.tensor_scalar(stat[:, 0, :], stat[:, 0, :], 1.0 / D, None, ALU.mult))
                own.step(nc.vector.tensor_tensor(h[:, :, :], src[:, :, :], bcast(stat[:, 0, :], D), ALU.subtract))
                own.step(nc.vector.tensor_tensor(lnt[:, :, :], h[:, :, :], h[:, :, :], ALU.mult))
                own.step(nc.vector.reduce_sum(stat[:, 1, :], lnt[:, :, :], axis=AX))
                nc.vector.tensor_scalar(stat[:, 1, :], stat[:, 1, :], 1.0 / D, 1e-5, ALU.mult, ALU.add).then_inc(var_sem, 1)
                dve.wait_ge(std_sem, 1)
                own.step(nc.vector.reciprocal(stat[:, 0, :], stat[:, 1, :]))
                own.step(nc.vector.tensor_tensor(h[:, :, :], h[:, :, :], bcast(stat[:, 0, :], D), ALU.mult))
                return nc.vector.tensor_scalar(h[:, :, :], h[:, :, :], 0.0, None, ALU.max)

            dve.wait_ge(nat_in, 32)
            nc.vector.tensor_copy(natf[:, 0, :], nat[:, :, 0])
            own.link(nc.vector.tensor_copy(natf[:, 1, :], nat[:, :, 1]))
            own.link(nc.vector.tensor_scalar(dblk[:, :], nat[:, :, 1], 7, None, ALU.arith_shift_right))
            own.wait()
            nc.vector.tensor_copy(dblkf[:, :], dblk[:, :])
            nc.vector.memset(row_nextf[:, :], float(FAR))
            nc.vector.memset(viol[:, :], 0.0).then_inc(nat_ready, 1)
            dve.wait_ge(nat_ready, 1)
            own.step(nc.vector.tensor_copy(row_nextf[0:NP - 1, :], row_next[0:NP - 1, 1:2]))
            own.step(nc.vector.tensor_tensor(junk_d[:, 0:NC - 1], natf[:, 1, 1:NC], natf[:, 1, 0:NC - 1], ALU.is_lt))
            own.step(nc.vector.reduce_sum(viol[:, 0:1], junk_d[:, 0:NC - 1], axis=AX))
            own.step(nc.vector.tensor_tensor(viol[:, 1:2], row_nextf[:, :], natf[:, 1, NC - 1:NC], ALU.is_lt))
            nc.vector.tensor_tensor(viol[:, 2:3], viol[:, 0:1], viol[:, 1:2], ALU.add).then_inc(viol_ready, 1)

            dve.wait_ge(x_in, 32)
            norm_relu(xs, var_ready, std_ready).then_inc(h_ready, 1)

            dve.wait_ge(consts, 1)
            def count_dst(b, first):
                if not first:
                    dve.wait_ge(d_cum, b)
                nc.vector.tensor_scalar(junk_d[:, :], natf[:, 1, :], thr[0:NP, bass.ds(b, 1)], 0.0, ALU.is_lt, ALU.add,
                                        accum_out=cum[:, 1, bass.ds(b + 1, 1)]).then_inc(d_cum, 1)
            count_dst(0, True)
            with dve.Fori(1, NB) as b:
                count_dst(b, False)
            dve.wait_ge(d_cum, NB)

            for n, k in enumerate((1, 0)):
                if k == 0:
                    dve.wait_ge(s_cum, NB)
                    own.step(nc.vector.tensor_scalar(cum[:, 0, 1:NB + 1], ssum[:, :], float(NC), 0.5, ALU.add, ALU.mult))
                nc.vector.tensor_tensor(cnt[:, k, :], cum[:, k, 1:NB + 1], cum[:, k, 0:NB], ALU.subtract).then_inc(cnt_ready, 1)
                dve.wait_ge(n_ready, n + 1)
                own.step(nc.vector.tensor_copy(ncol[:, k:k + 1], pb[3][0:NB, 0:1]))
                own.step(nc.vector.tensor_scalar(tcol_i[:, k:k + 1], ncol[:, k:k + 1], float(P - 1), None, ALU.add))
                own.step(nc.vector.tensor_scalar(tcol_i[:, k:k + 1], tcol_i[:, k:k + 1], 7, None, ALU.arith_shift_right))
                nc.vector.tensor_copy(tcol[:, k:k + 1], tcol_i[:, k:k + 1]).then_inc(tiles_ready, 1)
                dve.wait_ge(tiles_ready, n + 1)
                own.step(nc.vector.scalar_tensor_tensor(slack[:, k:k + 1], tcol[:, k:k + 1], -float(P), ncol[:, k:k + 1],
                                                        op0=ALU.mult, op1=ALU.add))
                dve.wait_ge(tend_ready, n + 1)
                own.step(nc.vector.tensor_copy(tend[:, k:k + 1], pb[3][0:NB, 1:2]))
                nc.vector.tensor_scalar(ge[:, :], jrow[:, :], tend[:, k:k + 1], None, ALU.is_ge).then_inc(ge_ready, 1)
                for c in range(J // JC):
                    dve.wait_ge(sched_ps, n * (J // JC) + c + 1)
                    s = slice(c * JC, (c + 1) * JC)
                    nc.vector.tensor_copy(base_row[k][:, s], pb[4][:, 0:JC])
                    own.link(nc.vector.tensor_scalar(e0f[:, s], pb[5][0:1, 0:JC], 1.0, None, ALU.mult))
                    nc.vector.tensor_copy(blk[k][:, s], pb[6][0:1, 0:JC]).then_inc(sched_read, 1)
                own.wait()
                own.step(nc.vector.scalar_tensor_tensor(e0f[:, :], jrow[0:1, :], float(P), e0f[:, :], op0=ALU.mult, op1=ALU.add))
                nc.vector.tensor_scalar(e0[k][:, :], e0f[:, :], float(E), None, ALU.min).then_inc(sched_done, 1)
                if k == 1:
                    dve.wait_ge(fbase_ps, 1)
                    nc.vector.tensor_copy(fb_base, pb[7][0:NP, 0:NB]).then_inc(fbase_ready, 1)
                    dve.wait_ge(flag_ps, 1)
                    nc.vector.tensor_copy(flag[:, :], pb[7][0:1, 256:257]).then_inc(flag_ready, 1)
            dve.wait_ge(rearranged, 1)
            dve.wait_ge(sched_read, 2 * (J // JC))
            own.step(nc.vector.memset(acc[:, :, :], 0.0))
            dve.wait_ge(sched_done, 2)

            dve.wait_ge(begin_ps, 1)
            own.step(nc.vector.tensor_copy(q_row[:, 0, :], pb[7][:, 0:NB]))

            chain = Chain(dve, dve_d)
            q = pb[4][:, 0:(U + 1) * NB].rearrange("p (u b) -> p u b", b=NB)

            def small_of(r):
                return [small[:, r % 2, m, :] for m in range(7)]

            def dst_row(i, r):
                dloc = small_of(r)[0]
                dve.wait_ge(ld_sd[r], 16 * U * (i + 1))
                floats = chain.link(nc.vector.tensor_copy(sdf[:, r % 2, :, :], rec_i[:, r, :, :]))
                blocks = chain.link(nc.vector.tensor_scalar(sblk[:, r % 2, :], rec_i[:, r, :, 0], 7, None, ALU.arith_shift_right))
                chain.wait(floats)
                row = chain.link(nc.vector.tensor_tensor(dloc, sdf[:, r % 2, :, 1], base_row[1][:, bass.ds(i * (U * R) + r * U, U)], ALU.subtract))
                return row

            def dst_one_hot(r, row):
                dloc, clamp, valid, key, off, skey, _ = small_of(r)
                chain.wait(row)
                nc.vector.tensor_tensor(ohd[:, r % 2, :, :], bcast_mid(iota128[:, :], U), bcast(dloc, P), ALU.is_equal).then_inc(ohd_ready, 1)
                clamped = chain.link(nc.vector.tensor_scalar(clamp, dloc, 0.0, float(P - 1), ALU.max, ALU.min))
                chain.link(nc.vector.tensor_scalar(skey, sblk[:, r % 2, :], 1.0, None, ALU.add))
                return clamped

            def src_one_hot(r, clamped):
                dloc, clamp, valid, key, off, skey, _ = small_of(r)
                chain.wait(clamped)
                chain.step(nc.vector.tensor_tensor(valid, clamp, dloc, ALU.is_equal))
                keyed = chain.link(nc.vector.tensor_tensor(key, skey, valid, ALU.mult))
                chain.link(nc.vector.tensor_scalar(off, valid, -BIG, BIG, ALU.mult, ALU.add))
                chain.wait(keyed)
                nc.vector.tensor_tensor(ohs[:, r % 2, :, :], bcast_mid(iota_blk1[:, :], U), bcast(key, NB), ALU.is_equal).then_inc(ohs_ready, 1)

            def add_step(dst, at, src, width, u):
                to = dst[:, bass.ds(at[u], 1), :].rearrange("p a c -> p (a c)")
                return nc.vector.tensor_tensor(to, to, src[:, u * width:(u + 1) * width], ALU.add)

            def add_steps(dst, k, src, width, i, r, ready, done, links, first):
                v = i * R + r + 1
                at = four(dve, blk[k], i * (U * R) + r * U, NB)
                if not (first and r == 0):
                    dve.wait_ge(done, v - 1)
                    dve.sem_inc(dve_tick, 1)
                dve.wait_ge(ready, v)
                for u in range(U - 1):
                    links.step(add_step(dst, at, src, width, u))
                add_step(dst, at, src, width, U - 1).then_inc(done, 1)

            def positions(i, r, first):
                v = i * R + r + 1
                off, p = small_of(r)[4], small_of(r)[6]
                if not first:
                    dve.wait_ge(sct[r], 16 * U * i)
                    dve.sem_inc(dve_tick, 1)
                dve.wait_ge(q_ready, v)
                placed = chain.link(nc.vector.tensor_tensor(prod[:, :, :], q[:, 0:U, :], bcast_mid(q_row[:, r % 2, :], U), ALU.add))
                nc.vector.tensor_tensor(q_row[:, (r + 1) % 2, :], q_row[:, r % 2, :], q[:, U, :], ALU.add).then_inc(q_read, 1)
                chain.wait(placed)
                chain.link(nc.vector.tensor_tensor(prod[:, :, :], prod[:, :, :], ohs[:, r % 2, :, :], ALU.mult))
                chain.wait()
                chain.step(nc.vector.reduce_sum(p, prod[:, :, :], axis=AX))
                nc.vector.tensor_tensor(pos[:, r, :], p, off, ALU.add).then_inc(pos_ready, 1)

            def add_and_prepare(i, r, first, ahead):
                v = i * R + r + 1
                at = four(dve, blk[1], i * (U * R) + r * U, NB)
                if not (first and r == 0):
                    dve.wait_ge(acc_done, v - 1)
                    dve.sem_inc(dve_tick, 1)
                dve.wait_ge(sum_ready, v)
                added = chain.link(add_step(acc, at, pb[3], ACC, 0))
                row = dst_row(*ahead) if ahead else None
                chain.wait(added)
                added = chain.link(add_step(acc, at, pb[3], ACC, 1))
                clamped = dst_one_hot(ahead[1], row) if ahead else None
                chain.wait(added)
                added = chain.link(add_step(acc, at, pb[3], ACC, 2))
                if ahead:
                    src_one_hot(ahead[1], clamped)
                chain.wait(added)
                add_step(acc, at, pb[3], ACC, 3).then_inc(acc_done, 1)

            assert U == 4
            per = R * (8 + 3 + 3)

            def edges(i, first, last):
                chain.n, chain.base = FRONT, i * per
                for r in range(R):
                    positions(i, r, first)
                    ahead = (i, r + 2) if r < R - 2 else None if last else (i + 1, r + 2 - R)
                    add_and_prepare(i, r, first, ahead)
                assert last or chain.n == FRONT + per, (chain.n, FRONT, per)
            for r in range(2):
                src_one_hot(r, dst_one_hot(r, dst_row(0, r)))
            FRONT = chain.n
            assert FRONT == 16
            rounds(dve, edges)

            schain = Chain(dve, dve_s)

            def src_one_hots(i, r):
                cols = bass.ds(i * (U * R) + r * U, U)
                dve.wait_ge(ld_srec[r], 16 * U * (i + 1))
                schain.link(nc.vector.tensor_copy(ssrc[:, r % 2, :], srec[:, r, :, HID + 1].bitcast(I32)))
                nc.vector.tensor_scalar(dcol[:, cols], srec[:, r, :, HID + 2].bitcast(I32), 0, None, ALU.bitwise_or)
                schain.wait()
                schain.step(nc.vector.tensor_tensor(sloc[:, cols], ssrc[:, r % 2, :], base_row[0][:, cols], ALU.subtract))
                nc.vector.tensor_tensor(ohd[:, r % 2, :, :], bcast_mid(iota128[:, :], U), bcast(sloc[:, cols], P), ALU.is_equal).then_inc(soh_ready, 1)

            def sums(i, first, last):
                per_s = R * 5
                schain.n, schain.base = 2, i * per_s
                for r in range(R):
                    if r < R - 1:
                        src_one_hots(i, r + 1)
                    elif not last:
                        src_one_hots(i + 1, 0)
                    add_steps(acc, 0, pb[5 + r % 2], ACC, i, r, ssum_ready, sacc_done, schain, first)
                assert last or schain.n == 2 + per_s
            src_one_hots(0, 0)
            rounds(dve, sums)

            dve.wait_ge(b1_ready, 1)
            own.step(nc.vector.tensor_copy(bn2b[:, :], pb[7][:, 0:D]))
            own.step(nc.vector.tensor_tensor(xs[:, :, :], xs[:, :, :], bcast_mid(bn2b[:, :], NBP), ALU.add))

            def nodes(i):
                dve.wait_ge(outp_ps, i + 1)
                to = xs[:, bass.ds(i * U, U), :]
                nc.vector.tensor_tensor(to, to, pb[3][:, 0:U * D].rearrange("p (u f) -> p u f", u=U), ALU.add).then_inc(x1_done, 1)
            nodes(0)
            with dve.Fori(1, NBP // U) as i:
                nodes(i)
            dve.wait_ge(x1_done, NBP // U)
            norm_relu(xs, var2_ready, std2_ready).then_inc(h2_ready, 1)

            gchain = Chain(dve, dve_g)
            dve.wait_ge(acc2_zero, 1)

            def neighbour_one_hots(i, r):
                cols = bass.ds(i * (U * R) + r * U, U)
                nc.vector.tensor_tensor(ohd[:, r % 2, :, :], bcast_mid(iota128[:, :], U), bcast(sloc[:, cols], P), ALU.is_equal).then_inc(noh_ready, 1)

            def neighbours(i, first, last):
                gchain.n, gchain.base = 0, i * R * 3
                for r in range(R):
                    if r < R - 1:
                        neighbour_one_hots(i, r + 1)
                    elif not last:
                        neighbour_one_hots(i + 1, 0)
                    add_steps(acc2, 0, pb[5 + r % 2], D, i, r, nsum_ready, nacc_done, gchain, first)
            neighbour_one_hots(0, 0)
            rounds(dve, neighbours)
            dve.wait_ge(nacc_done, NI * R)
            nc.vector.tensor_tensor(lnt[:, :, :], xs[:, :, :], acc2[:, :, :], ALU.add).then_inc(y_ready, 1)


N_W = 16 + 10 + 6


def kernel(**inputs):
    import numpy as np
    import concourse.bacc as bacc
    from concourse.bass_utils import run_bass_kernel_spmd

    nc = bacc.Bacc("TRN2", target_bir_lowering=False, num_devices=1)
    laid = {"x": inputs["x"], "sd": np.stack([inputs["src"], inputs["dst"]], axis=1), "ea": inputs["edge_attr_16"]}
    for name in ("Wf1", "bf1", "Wf2", "bf2", "Wn1", "bn1", "Wn2", "bn2"):
        laid[name] = inputs[f"L0_gnn_{name}"]
    arrays, args = {}, []
    for name, a in laid.items():
        a = np.ascontiguousarray(a)
        arrays[f"in_{name}"] = a
        args.append(nc.dram_tensor(f"in_{name}", a.shape, mybir.dt.from_np(a.dtype), kind="ExternalInput").ap())
    args.append(nc.dram_tensor("out_x", (N, D), F32, kind="ExternalOutput").ap())
    build(nc, *args)
    r = run_bass_kernel_spmd(nc, [arrays], core_ids=[0])
    return r.results[0]["out_x"]
```

```python
from contextlib import ExitStack

import concourse.bass as bass
from concourse import mybir

P = 128
F32 = mybir.dt.float32
BF16 = mybir.dt.bfloat16
I32 = mybir.dt.int32
U32 = mybir.dt.uint32
ALU = mybir.AluOpType
ACT = mybir.ActivationFunctionType
AX = mybir.AxisListType.X

N, D, E, EA, HID = 12500, 32, 200000, 16, 64
NB = -(-N // P)
U = 4
R = 4
NBP = -(-(NB + 1) // (2 * U)) * 2 * U
NG = NBP // U
W = U * R
NI = -(-(-(-E // P) + NB) // W)
J = NI * W
EP = (-(-E // P) + W) * P
NP, NC = 125, E // 125
REC = HID + 3
ACC = HID + 1
FAR = 32768
BIG = float(1 << 22)
JC = J // 4
N_ACT = 46
SW = 4
assert E % 125 == 0 and JC <= 512 and J % 4 == 0 and NI % SW == 0


class Chain:

    def __init__(self, eng, sem, tick=None):
        self.eng, self.sem, self.n, self.base, self.tick = eng, sem, 0, 0, tick

    def link(self, ins):
        self.n += 1
        ins.then_inc(self.sem, 1)
        return self.n

    def wait(self, mark=None):
        self.eng.wait_ge(self.sem, self.base + (self.n if mark is None else mark))
        if self.tick is not None:
            self.eng.sem_inc(self.tick, 1)

    def step(self, ins):
        self.link(ins)
        self.wait()


def bcast(ap, n):
    return ap.unsqueeze(2).broadcast_to([ap.shape[0], ap.shape[1], n])


def bcast_mid(ap, n):
    return ap.unsqueeze(1).broadcast_to([ap.shape[0], n, ap.shape[1]])


def build(nc, x, sd, ea, Wf1, bf1, Wf2, bf2, Wn1, bn1, Wn2, bn2, out):
    with ExitStack() as ctx:
        def sb(name, shape, dt=F32):
            return ctx.enter_context(nc.sbuf_tensor(name, shape, dt))

        def sem(name):
            return ctx.enter_context(nc.semaphore(name))

        def sems(name, n):
            return [sem(f"{name}{i}") for i in range(n)]

        def dram(name, shape, dt=F32):
            return nc.dram_tensor(name, shape, dt).ap()

        by_d_sd = dram("by_d_sd", [EP, 2], I32)
        by_d_ea = dram("by_d_ea", [EP, EA])
        t2_rows = dram("t2_rows", [NBP * P, P])
        records = dram("records", [EP, REC])
        h2_rows = dram("h2_rows", [NBP * P, D])

        iota128 = sb("iota128", [P, P])
        iota_blk1 = sb("iota_blk1", [P, NB])
        ones = sb("ones", [P, P])
        ident = sb("ident", [P, P])
        before = sb("before", [P, P])
        upto = sb("upto", [P, P])
        ones_h = sb("ones_h", [P, P], BF16)
        before_h = sb("before_h", [P, P], BF16)
        tail_sd = sb("tail_sd", [P, 2], I32)
        tail_rec = sb("tail_rec", [P, REC])
        w12 = sb("w12", [P, U, 2 * P])
        wee = sb("wee", [EA + 1, P])
        wf2e = sb("wf2e", [ACC, HID])
        wf2T = sb("wf2T", [HID, ACC])
        wflow = sb("wflow", [ACC, HID])
        wn1 = sb("wn1", [HID, HID])
        bn1c = sb("bn1c", [HID, 1])
        wn2 = sb("wn2", [HID, D])
        bn2r = sb("bn2r", [1, D])
        xs = sb("xs", [P, NBP, D])
        h = sb("h", [P, NBP, D])
        lnt = sb("lnt", [P, NBP, D])
        stat = sb("stat", [P, 2, NBP])
        t1 = sb("t1", [P, NBP, P])
        acc = sb("acc", [P, NBP, ACC])
        acc_flat = acc[:, :, :].rearrange("p b c -> p (b c)")
        jrow = acc_flat[0:NB, 0:J]
        ge = acc_flat[0:NB, J:J + J // 2].bitcast(BF16)
        nblk = acc_flat[0:NP, 2 * J:2 * J + NC].bitcast(BF16).rearrange("p (k c) -> p k c", k=2)
        assert 2 * J + NC <= NBP * ACC
        acc2 = t1[:, 0:NG, :].rearrange("p b (u f) -> p (b u) f", f=D)
        t1_rest = t1[:, NG:NBP, :].rearrange("p b c -> p (b c)")
        srec = [t1_rest[:, w * W * REC:(w + 1) * W * REC].rearrange("p (t c) -> p t c", c=REC) for w in range(SW)]
        at_ = SW * W * REC
        accs = t1_rest[:, at_:at_ + 2 * U * ACC].rearrange("p (k u c) -> p k u c", k=2, u=U)
        at_ += 2 * U * ACC
        accT = t1_rest[0:ACC, at_:at_ + 2 * U * P].rearrange("p (k n) -> p k n", k=2)
        at_ += 2 * U * P
        nodeT = t1_rest[0:HID, at_:at_ + 2 * U * P].rearrange("p (k n) -> p k n", k=2)
        at_ += 2 * U * P
        assert at_ <= (NBP - NG) * P
        hs = sb("hs", [P, 2, P])
        hT = sb("hT", [P, 2, P])
        t2s = sb("t2s", [P, 2, U, P])
        raw = sb("raw", [P, 2, J], I32)
        nat = raw[:, :, :].rearrange("p k j -> p (k j)")[0:NP, 0:2 * NC].rearrange("p (c k) -> p c k", k=2)
        pairs = raw[:, :, :].rearrange("p k j -> p (k j)").bitcast(F32).rearrange("p (j k) -> p j k", k=2)
        wide = sb("wide", [P, 2, J])
        base_row = [wide[:, k, :] for k in range(2)]
        blk_i = lnt[0:NP, 0:NC // D, :].rearrange("p b f -> p (b f)").bitcast(I32)
        assert NC % D == 0
        e0f = lnt[0:1, 0:J // D, :].rearrange("p b f -> p (b f)")
        junk_d = sb("junk_d", [NP, NC], BF16)
        half_blk = sb("half_blk", [NP, N_ACT])
        row_next = sb("row_next", [NP, 2], I32)
        row_nexti = sb("row_nexti", [NP, 1], I32)
        row_nextf = sb("row_nextf", [NP, 1])
        viol = sb("viol", [NP, 3])
        flag = sb("flag", [1, 1], I32)
        cum = sb("cum", [NP, 2, NB + 1])
        cnt = sb("cnt", [NP, NB])
        edge_col = sb("edge_col", [NB, 4])
        edge_coli = sb("edge_coli", [NB, 3], I32)
        tile_col = sb("tile_col", [NB, 4])
        tcol = sb("tcol", [NB, 2])
        tend = sb("tend", [NB, 2])
        slack = sb("slack", [NB, 2])
        slack_h = sb("slack_h", [NB, 2], BF16)
        c128 = sb("c128", [NB, P], BF16)
        sched = sb("sched", [P, J], I32)
        e0 = [sched[32 * k:32 * k + 1, :] for k in (0, 1)]
        window = sb("window", [1, NI], I32)
        blk = [sched[32 * k:32 * k + 1, :] for k in (2, 3)]
        rec = sb("rec", [P, R, U, REC])
        rec_i = sb("rec_i", [P, R, U, 2], I32)
        eat = sb("eat", [P, R, U, EA + 1])
        g2 = sb("g2", [P, R, U, P])
        sdf = sb("sdf", [P, 2, U, 2])
        small = sb("small", [P, 2, 7, U])
        sblk = sb("sblk", [P, 2, U], I32)
        ohd = sb("ohd", [P, 2, U, P])
        ohs = sb("ohs", [P, 2, U, NB], BF16)
        prod = sb("prod", [P, U, NB])
        pos = sb("pos", [P, R, U], I32)
        q_row = sb("q_row", [P, 2, NB])
        oht = sb("oht", [P, 2, U, P])
        eaT = sb("eaT", [EA + 1, 2, U, P])
        rf = sb("rf", [P, U, ACC])
        junk_of = {"dve": [junk_d[:, :], oht[:, :, :, :].rearrange("p k u n -> p (k u n)").bitcast(BF16)[0:NP, 0:NC]],
                   "act": [t[:, :, :, :].rearrange("p k u n -> p (k u n)").bitcast(BF16)[0:NP, 0:NC] for t in (ohd, g2)]}
        s_oh = [ohd[:, 0, :, :], ohd[:, 1, :, :], oht[:, 0, :, :], oht[:, 1, :, :]]
        didx = sb("didx", [P, R, U], I32)
        h2g = sb("h2g", [P, R, U, D])
        bn2b = sb("bn2b", [P, D])

        fb_base = sb("fb_base", [NP, NB])[:, :]
        fb_blk = sb("fb_blk", [NP, 1])
        fb_oh = sb("fb_oh", [NP, NB])
        fb_prod = sb("fb_prod", [NP, P])
        fb_pos = sb("fb_pos", [NP, 1])
        fb_posi = sb("fb_posi", [NP, 1], I32)
        fb_sd = sb("fb_sd", [NP, 2], I32)
        fb_ea = sb("fb_ea", [NP, EA])
        fb_own = sem("fb_own")

        pb = [ctx.enter_context(nc.psum_tensor(f"bank{i}", [P, 512], F32)) for i in range(8)]

        x_in, w_in, nat_in = sem("x_in"), sem("w_in"), sem("nat_in")
        by_d_copied = sem("by_d_copied")
        tails_set = sem("tails_set")
        consts = sem("consts")
        pool_own, dve_own, act_own = sem("pool_own"), sem("dve_own"), sem("act_own")
        rearranged = sem("rearranged")
        var_ready, std_ready, h_ready = sem("var_ready"), sem("std_ready"), sem("h_ready")
        hs_ready, hsT_ready, hT_ready, tab_ready = sem("hs_ready"), sem("hsT_ready"), sem("hT_ready"), sem("tab_ready")
        t1_ready, t2s_ready, t2_written = sem("t1_ready"), sem("t2s_ready"), sems("t2_written", 2)
        b1_ready = sem("b1_ready")
        nblk_ready, cum_act = sem("nblk_ready"), sem("cum_act")
        cum_ready = sem("cum_ready")
        cnt_ready, n_ready, tiles_ready, tend_ready = sem("cnt_ready"), sem("n_ready"), sem("tiles_ready"), sem("tend_ready")
        ge_ready, sched_ps, sched_read, sched_done = sem("ge_ready"), sem("sched_ps"), sem("sched_read"), sem("sched_done")
        viol_ready, flag_ps, flag_ready = sem("viol_ready"), sem("flag_ps"), sem("flag_ready")
        begin_ps = sem("begin_ps")
        fbase_ps, fbase_ready = sem("fbase_ps"), sem("fbase_ready")
        fb_ld, fb_sc = sem("fb_ld"), sems("fb_sc", 2)
        ld_sd, ld_ea, gat, sct = sems("ld_sd", R), sems("ld_ea", R), sems("gat", R), sems("sct", R)
        ohd_ready, ohs_ready, tp_ready, oht_ready = sem("ohd_ready"), sem("ohs_ready"), sem("tp_ready"), sem("oht_ready")
        q_ready, q_read, pos_ready = sem("q_ready"), sem("q_read"), sem("pos_ready")
        pre_ready, relu_ready, sum_ready, acc_done = sem("pre_ready"), sem("relu_ready"), sem("sum_ready"), sem("acc_done")
        pool_tick, act_tick, pe_tick, dve_tick = sem("pool_tick"), sem("act_tick"), sem("pe_tick"), sem("dve_tick")
        dve_d = sem("dve_d")
        ld_srec = sems("ld_srec", SW)
        pair_ready, soh_ready, ssum_ready, sacc_done, dve_s = sem("pair_ready"), sem("soh_ready"), sem("ssum_ready"), sem("sacc_done"), sem("dve_s")
        accs_ready, accT_ps, accT_ready = sem("accs_ready"), sem("accT_ps"), sem("accT_ready")
        wf2T_ps, wf2T_ready, wflow_ps, wflow_ready = sem("wf2T_ps"), sem("wf2T_ready"), sem("wflow_ps"), sem("wflow_ready")
        node_ps, node_ready = sem("node_ps"), sem("node_ready")
        outp_ps, x1_done, dve_n = sem("outp_ps"), sem("x1_done"), sem("dve_n")
        var2_ready, std2_ready, h2_ready, h2_written = sem("var2_ready"), sem("std2_ready"), sem("h2_ready"), sem("h2_written")
        didx_ready, gh = sem("didx_ready"), sems("gh", R)
        noh_ready, nsum_ready, nacc_done, dve_g = sem("noh_ready"), sem("nsum_ready"), sem("nacc_done"), sem("dve_g")
        acc2_zero, y_ready, y_out = sem("acc2_zero"), sem("y_ready"), sem("y_out")

        sched_bank = [3, 5]
        s_bank = [pb[5], pb[6], pb[2], pb[3]]
        block = ctx.enter_context(nc.Block())
        N_FULL = N // P
        N_TAIL = N - N_FULL * P

        def four(eng, row, j0, top):
            return nc.values_load_multi_w_load_instructions(
                row[0:1, bass.ds(j0, U)], engines=[eng.engine], min_val=0, max_val=top,
                skip_runtime_bounds_check_because="the schedule clamps it to this range")[1]

        def window_of(eng, row, j0, top):
            return nc.values_load_multi_w_load_instructions(
                row[0:1, bass.ds(j0, W)], engines=[eng.engine], min_val=0, max_val=top,
                skip_runtime_bounds_check_because="the schedule clamps it to this range")[1]

        def rounds(eng, body):
            body(0, True, False)
            with eng.Fori(1, NI - 1) as i:
                body(i, False, False)
            body(NI - 1, False, True)

        def rounds_of(eng, n, body):
            body(0, True, False)
            with eng.Fori(1, n - 1) as i:
                body(i, False, False)
            body(n - 1, False, True)

        @block.sync
        def _(sp):
            sp.dma_start(nat[:, :, :], sd.rearrange("(p c) k -> p c k", p=NP)).then_inc(nat_in, 16)
            sp.dma_start(row_next[0:NP - 1, :], sd.rearrange("(p c) k -> p c k", p=NP)[1:NP, 0, :]).then_inc(nat_in, 16)
            sp.dma_start(xs[:, 0:N_FULL, :], x[0:N_FULL * P, :].rearrange("(b p) f -> p b f", p=P)).then_inc(x_in, 16)
            sp.wait_ge(tails_set, 1)
            sp.dma_start(xs[0:N_TAIL, N_FULL, :], x[N_FULL * P:N, :]).then_inc(x_in, 16)
            n_w = 0
            for u in range(U):
                for c, r0 in enumerate((0, D, D, 0)):
                    sp.dma_start(w12[u * D:(u + 1) * D, u, c * HID:(c + 1) * HID], Wf1[r0:r0 + D, :]).then_inc(w_in, 16)
                    n_w += 1
            for c in range(2):
                sp.dma_start(wee[0:EA, c * HID:(c + 1) * HID], Wf1[2 * D:2 * D + EA, :]).then_inc(w_in, 16)
                sp.dma_start(wee[EA:EA + 1, c * HID:(c + 1) * HID], bf1.unsqueeze(0)).then_inc(w_in, 16)
                n_w += 2
            for dst_, src_ in ((wf2e[0:HID, :], Wf2), (wf2e[HID:ACC, :], bf2.unsqueeze(0)), (wn1[:, :], Wn1),
                               (bn1c[:, :], bn1.unsqueeze(1)), (wn2[:, :], Wn2), (bn2r[:, :], bn2.unsqueeze(0))):
                sp.dma_start(dst_, src_).then_inc(w_in, 16)
                n_w += 1
            assert n_w == N_W
            for to, of in ((by_d_sd, sd), (by_d_ea, ea)):
                sp.dma_start(to[0:E, :].rearrange("(p c) f -> p (c f)", p=1600),
                             of.rearrange("(p c) f -> p (c f)", p=1600)).then_inc(by_d_copied, 16)
            for to, of in ((by_d_sd, tail_sd[:, :]), (by_d_ea, tail_rec[:, 0:EA]), (records, tail_rec[:, :])):
                sp.dma_start(to[E:EP - W * P, :], of[0:EP - W * P - E, :]).then_inc(by_d_copied, 16)
                sp.dma_start(to[EP - W * P:EP, :].rearrange("(t p) f -> p t f", p=P), bcast_mid(of, W)).then_inc(by_d_copied, 16)

            def store_t2(i, first, last):
                for k in range(2):
                    sp.wait_ge(t2s_ready, i * 2 + k + 1)
                    sp.dma_start(t2_rows[bass.ds((i * 2 + k) * (U * P), U * P), :].rearrange("(u p) f -> p u f", p=P),
                                 t2s[:, k, :, :]).then_inc(t2_written[k], 16)
            rounds_of(sp, NG // 2, store_t2)

            sp.wait_ge(sched_done, 1)
            sp.wait_ge(rearranged, 1)

            def load_edges(i, first, last):
                for r in range(R):
                    at = four(sp, e0[1], i * W + r * U, EP - W * P)
                    if not first:
                        sp.wait_ge(relu_ready, i * R + r + 1 - R)
                    for u in range(U):
                        sp.dma_start(rec_i[:, r, u, :], by_d_sd[bass.ds(at[u], P), :]).then_inc(ld_sd[r], 16)
                    for u in range(U):
                        sp.dma_start(eat[:, r, u, 0:EA], by_d_ea[bass.ds(at[u], P), :]).then_inc(ld_ea[r], 16)
            rounds(sp, load_edges)

            sp.wait_ge(sched_done, 2)
            for r in range(R):
                sp.wait_ge(sct[r], 16 * U * NI)

            def load_records(i, first, last):
                for w in range(SW):
                    at = nc.values_load_multi_w_load_instructions(
                        window[0:1, bass.ds(i * SW + w, 1)], engines=[sp.engine], min_val=0, max_val=EP - W * P,
                        skip_runtime_bounds_check_because="the schedule clamps it to this range")[1][0]
                    if not first:
                        sp.wait_ge(ssum_ready, (i * SW + w + 1) * R - SW * R)
                    sp.dma_start(srec[w], records[bass.ds(at, W * P), :].rearrange("(t p) c -> p t c", p=P)).then_inc(ld_srec[w], 16)
            rounds_of(sp, NI // SW, load_records)

            sp.wait_ge(h2_ready, 1)
            sp.dma_start(h2_rows.rearrange("(b p) f -> p b f", p=P), h[:, :, :]).then_inc(h2_written, 16)
            sp.wait_ge(y_ready, 1)
            sp.dma_start(out[0:N_FULL * P, :].rearrange("(b p) f -> p b f", p=P), lnt[:, 0:N_FULL, :]).then_inc(y_out, 16)
            sp.dma_start(out[N_FULL * P:N, :], lnt[0:N_TAIL, N_FULL, :]).then_inc(y_out, 16)
            sp.wait_ge(y_out, 32)
            sp.wait_ge(h2_written, 16)
            sp.wait_ge(by_d_copied, 16 * 8)
            for k in range(2):
                sp.wait_ge(t2_written[k], 16 * (NG // 2))

        FB_STEPS = 13

        def rearrange_edges(pool):
            ea_cols = ea.rearrange("(p c) f -> p c f", p=NP)
            last_row = pool.to_reg(E - 1)

            def column(c):
                own = Chain(pool, fb_own, pool_tick)
                own.base = c * FB_STEPS
                pool.dma_start(fb_ea[:, :], ea_cols[:, bass.ds(c, 1), :].rearrange("p a f -> p (a f)")).then_inc(fb_ld, 16)
                own.link(nc.gpsimd.tensor_copy(fb_blk[:, :], nblk[:, 1, bass.ds(c, 1)]))
                own.link(nc.gpsimd.tensor_copy(fb_sd[:, :], nat[:, bass.ds(c, 1), :].rearrange("p a k -> p (a k)")))
                own.wait()
                own.step(nc.gpsimd.tensor_scalar(fb_oh[:, :], iota128[0:NP, 0:NB], fb_blk[:, 0:1], None, ALU.is_equal))
                own.step(nc.gpsimd.tensor_tensor(fb_prod[:, 0:NB], fb_oh[:, :], fb_base, ALU.mult))
                for w in (64, 32, 16, 8, 4, 2):
                    own.step(nc.gpsimd.tensor_tensor(fb_prod[:, 0:w], fb_prod[:, 0:w], fb_prod[:, w:2 * w], ALU.add))
                own.link(nc.gpsimd.tensor_tensor(fb_pos[:, :], fb_prod[:, 0:1], fb_prod[:, 1:2], ALU.add))
                own.step(nc.gpsimd.tensor_tensor(fb_base, fb_base, fb_oh[:, :], ALU.add))
                own.link(nc.gpsimd.tensor_copy(fb_posi[:, :], fb_pos[:, :]))
                own.wait()
                assert own.n == FB_STEPS
                pool.wait_ge(fb_ld, 16 * (c + 1))
                pool.sem_inc(pool_tick, 1)
                for k, (rows, to) in enumerate(((fb_sd, by_d_sd), (fb_ea, by_d_ea))):
                    nc.gpsimd.indirect_dma_start(
                        out=to, out_offset=bass.IndirectOffsetOnAxis(ap=fb_posi[:, :].bitcast(U32), axis=0),
                        in_=rows[:, :], in_offset=None, bounds_check=last_row, oob_is_err=False).then_inc(fb_sc[k], 16)
                for k in range(2):
                    pool.wait_ge(fb_sc[k], 16 * (c + 1))
                    pool.sem_inc(pool_tick, 1)
            with pool.Fori(0, NC) as c:
                column(c)

        @block.gpsimd
        def _(pool):
            nc.gpsimd.memset(xs[:, N_FULL:NBP, :], 0.0)
            nc.gpsimd.memset(tail_rec[:, 0:HID + 1], 0.0)
            nc.gpsimd.memset(w12[:, :, :], 0.0)
            nc.gpsimd.memset(fb_prod[:, :], 0.0)
            nc.gpsimd.memset(tail_sd[:, 0:1], 0)
            nc.gpsimd.memset(tail_sd[:, 1:2], FAR)
            nc.gpsimd.memset(tail_rec[:, HID + 1:HID + 2].bitcast(I32), FAR)
            nc.gpsimd.memset(tail_rec[:, HID + 2:HID + 3].bitcast(I32), 0).then_inc(tails_set, 1)
            own = Chain(pool, pool_own)
            nc.gpsimd.iota(iota128[:, :], [[1, P]], base=0, channel_multiplier=0, allow_small_or_imprecise_dtypes=True)
            nc.gpsimd.iota(iota_blk1[:, :], [[1, NB]], base=1, channel_multiplier=0, allow_small_or_imprecise_dtypes=True)
            nc.gpsimd.iota(jrow[:, :], [[1, J]], base=0, channel_multiplier=0, allow_small_or_imprecise_dtypes=True)
            nc.gpsimd.memset(ones[:, :], 1.0)
            nc.gpsimd.memset(ones_h[:, :], 1.0)
            nc.gpsimd.memset(c128[:, :], float(P))
            nc.gpsimd.memset(cum[:, :, 0:1], 0.0)
            nc.gpsimd.memset(rf[:, :, HID:ACC], 1.0)
            nc.gpsimd.memset(rec[:, :, :, HID:HID + 1], 1.0)
            own.step(nc.gpsimd.memset(eat[:, :, :, EA:EA + 1], 1.0))
            for m, op in ((before, ALU.is_gt), (upto, ALU.is_ge), (ident, ALU.is_equal), (before_h, ALU.is_gt)):
                ins = nc.gpsimd.affine_select(out=m[:, :], in_=ones[:, :], compare_op=op, fill=0.0, base=0,
                                              pattern=[[1, P]], channel_multiplier=-1)
            ins.then_inc(consts, 1)

            pool.wait_ge(by_d_copied, 16 * 8)
            pool.wait_ge(flag_ready, 1)
            pool.wait_ge(fbase_ready, 1)
            unsorted_edges = pool.value_load(flag[0:1, 0:1], min_val=0, max_val=1 << 20)
            with pool.If(unsorted_edges > 0):
                rearrange_edges(pool)
            with pool.Else():
                pool.sem_inc(pool_tick, 1)
            pool.sem_inc(rearranged, 1)

            for k in range(2):
                pool.wait_ge(t2_written[k], 16 * (NG // 2))
            pool.wait_ge(cum_act, N_ACT)
            end = pool.to_reg(E - 1)

            def gather_t2(i, r):
                pool.wait_ge(ld_sd[r], 16 * U * (i + 1))
                pool.sem_inc(pool_tick, 1)
                for u in range(U):
                    nc.gpsimd.indirect_dma_start(
                        out=g2[:, r, u, :], out_offset=None, in_=t2_rows,
                        in_offset=bass.IndirectOffsetOnAxis(ap=rec_i[:, r, u, 0:1].bitcast(U32), axis=0)).then_inc(gat[r], 16)

            def scatter_records(i, r):
                pool.wait_ge(pos_ready, i * R + r + 1)
                pool.sem_inc(pool_tick, 1)
                pool.wait_ge(relu_ready, i * R + r + 1)
                pool.sem_inc(pool_tick, 1)
                for u in range(U):
                    nc.gpsimd.indirect_dma_start(
                        out=records, out_offset=bass.IndirectOffsetOnAxis(ap=pos[:, r, u:u + 1].bitcast(U32), axis=0),
                        in_=rec[:, r, u, :], in_offset=None, bounds_check=end, oob_is_err=False).then_inc(sct[r], 16)

            def edges(i, first, last):
                for r in range(R):
                    if r < R - 2:
                        gather_t2(i, r + 2)
                    elif not last:
                        gather_t2(i + 1, r + 2 - R)
                    scatter_records(i, r)
            gather_t2(0, 0)
            gather_t2(0, 1)
            rounds(pool, edges)

            pool.wait_ge(pre_ready, NI * R)
            nc.gpsimd.memset(acc2[:, :, :], 0.0).then_inc(acc2_zero, 1)
            pool.wait_ge(h2_written, 16)

            def gather_h2(i, first, last):
                for r in range(R):
                    pool.wait_ge(didx_ready, i * R + r + 1)
                    pool.sem_inc(pool_tick, 1)
                    if not first:
                        pool.wait_ge(nsum_ready, i * R + r + 1 - R)
                        pool.sem_inc(pool_tick, 1)
                    for u in range(U):
                        nc.gpsimd.indirect_dma_start(
                            out=h2g[:, r, u, :], out_offset=None, in_=h2_rows,
                            in_offset=bass.IndirectOffsetOnAxis(ap=didx[:, r, u:u + 1].bitcast(U32), axis=0)).then_inc(gh[r], 16)
            rounds(pool, gather_h2)

        @block.scalar
        def _(act):
            act.wait_ge(var_ready, 1)
            nc.scalar.activation(stat[:, 1, :], stat[:, 1, :], ACT.Sqrt).then_inc(std_ready, 1)
            act.wait_ge(h_ready, 1)

            def stage_h(i, k, first):
                if not first:
                    act.wait_ge(hsT_ready, i * 2 + k - 1)
                    act.sem_inc(act_tick, 1)
                nc.scalar.activation(hs[:, k, :].rearrange("p (u f) -> p u f", u=U), h[:, bass.ds((i * 2 + k) * U, U), :], ACT.Copy).then_inc(hs_ready, 1)

            def tables(i, first, last):
                for k in range(2):
                    act.wait_ge(hsT_ready, i * 2 + k + 1)
                    nc.scalar.activation(hT[:, k, :], pb[k][:, 0:P], ACT.Copy).then_inc(hT_ready, 1)
                if not last:
                    for k in range(2):
                        stage_h(i + 1, k, False)
                for k in range(2):
                    act.wait_ge(tab_ready, i * 2 + k + 1)
                    act.sem_inc(act_tick, 1)
                    for n in range(2):
                        nc.scalar.activation(t1[:, bass.ds((i * 2 + k) * U + 2 * n, 2), :],
                                             pb[2 + 2 * k + n][:, :].rearrange("p (u c) -> p u c", u=2)[:, :, 0:P], ACT.Copy)
                    if not first:
                        act.wait_ge(t2_written[k], 16 * i)
                        act.sem_inc(act_tick, 1)
                    for n in range(2):
                        ins = nc.scalar.activation(t2s[:, k, 2 * n:2 * n + 2, :],
                                                   pb[2 + 2 * k + n][:, :].rearrange("p (u c) -> p u c", u=2)[:, :, P:2 * P], ACT.Copy)
                    ins.then_inc(t2s_ready, 1)
            for k in range(2):
                stage_h(0, k, True)
            rounds_of(act, NG // 2, tables)

            act.wait_ge(wf2T_ps, 1)
            nc.scalar.activation(wf2T[:, :], pb[7][0:HID, 0:ACC], ACT.Copy).then_inc(wf2T_ready, 1)
            act.wait_ge(wflow_ps, 1)
            nc.scalar.activation(wflow[:, :], pb[7][0:ACC, 0:HID], ACT.Copy).then_inc(wflow_ready, 1)

            def count_src(b, m, first):
                if not first:
                    act.wait_ge(cum_act, b - 1)
                    act.sem_inc(act_tick, 1)
                nc.scalar.activation(junk_of["act"][m], nblk[:, 0, :], ACT.Sign, bias=half_blk[:, bass.ds(b, 1)], scale=-1.0,
                                     accum_out=cum[:, 0, bass.ds(b + 1, 1)]).then_inc(cum_act, 1)
            act.wait_ge(nblk_ready, 1)
            for m in range(2):
                count_src(m, m, True)
            with act.Fori(1, N_ACT // 2) as i:
                for m in range(2):
                    count_src(i * 2 + m, m, False)

            def transposed(i, r):
                v = i * R + r + 1
                act.wait_ge(tp_ready, v)
                nc.scalar.activation(oht[:, r % 2, :, :].rearrange("p u n -> p (u n)"), pb[0][:, :], ACT.Copy)
                nc.scalar.activation(eaT[:, r % 2, :, :].rearrange("p u n -> p (u n)"), pb[1][0:EA + 1, :], ACT.Copy).then_inc(oht_ready, 1)

            def hidden(i, r, first):
                v = i * R + r + 1
                act.wait_ge(pre_ready, v)
                pre = pb[2][:, :].rearrange("p (u c) -> p u c", u=U)
                if not (first and r == 0):
                    act.wait_ge(sum_ready, v - 1)
                nc.scalar.activation(rf[:, :, 0:HID], pre[:, :, 0:HID], ACT.Relu)
                if not first:
                    act.wait_ge(sct[r], 16 * U * i)
                    act.sem_inc(act_tick, 1)
                nc.scalar.copy(rec[:, r, :, HID + 1:REC].bitcast(I32), rec_i[:, r, :, :])
                nc.scalar.activation(rec[:, r, :, 0:HID], pre[:, :, HID:P], ACT.Relu).then_inc(relu_ready, 1)

            def edges(i, first, last):
                for r in range(R):
                    hidden(i, r, first)
                    if r < R - 1:
                        transposed(i, r + 1)
                    elif not last:
                        transposed(i + 1, 0)
            transposed(0, 0)
            rounds(act, edges)

            def record_indices(i, first, last):
                for w in range(SW):
                    act.wait_ge(ld_srec[w], 16 * (i + 1))
                    act.sem_inc(act_tick, 1)
                    for r in range(R):
                        j0 = (i * SW + w) * W + r * U
                        at = four(act, e0[0], j0, W - 1)
                        for u in range(U):
                            ins = nc.scalar.copy(pairs[:, bass.ds(j0 + u, 1), :].rearrange("p a k -> p (a k)"),
                                                 srec[w][:, bass.ds(at[u], 1), HID + 1:REC].bitcast(I32).rearrange("p a k -> p (a k)"))
                        ins.then_inc(pair_ready, 1)
            rounds_of(act, NI // SW, record_indices)

            def stage_sums(i, k, first):
                if not first:
                    act.wait_ge(accT_ps, i * 2 + k - 1)
                    act.sem_inc(act_tick, 1)
                nc.scalar.activation(accs[:, k, :, :], acc[:, bass.ds((i * 2 + k) * U, U), :], ACT.Copy).then_inc(accs_ready, 1)

            def nodes(i, first, last):
                for k in range(2):
                    act.wait_ge(accT_ps, i * 2 + k + 1)
                    nc.scalar.activation(accT[:, k, :], pb[k][0:ACC, :], ACT.Copy).then_inc(accT_ready, 1)
                if not last:
                    for k in range(2):
                        stage_sums(i + 1, k, False)
                for k in range(2):
                    act.wait_ge(node_ps, i * 2 + k + 1)
                    nc.scalar.activation(nodeT[:, k, :], pb[2 + k][0:HID, :], ACT.Relu, bias=bn1c[:, :]).then_inc(node_ready, 1)
            act.wait_ge(sacc_done, NI * R)
            for k in range(2):
                stage_sums(0, k, True)
            rounds_of(act, NG // 2, nodes)
            act.wait_ge(var2_ready, 1)
            nc.scalar.activation(stat[:, 1, :], stat[:, 1, :], ACT.Sqrt).then_inc(std2_ready, 1)

            def indices(i, first, last):
                for r in range(R):
                    if not first:
                        act.wait_ge(gh[r], 16 * U * i)
                        act.sem_inc(act_tick, 1)
                    nc.scalar.copy(didx[:, r, :], pairs[:, bass.ds(i * W + r * U, U), 1]).then_inc(didx_ready, 1)
            rounds(act, indices)

        @block.tensor
        def _(pe):
            pe.wait_ge(consts, 1)
            pe.wait_ge(w_in, 16 * N_W)

            def transpose_h(i, k):
                pe.wait_ge(hs_ready, i * 2 + k + 1)
                nc.tensor.transpose(pb[k][:, 0:P], hs[:, k, :], ident[:, :]).then_inc(hsT_ready, 1)

            def tables(i, first, last):
                for k in range(2):
                    if not first:
                        pe.wait_ge(t2s_ready, i * 2 + k - 1)
                        pe.sem_inc(pe_tick, 1)
                    pe.wait_ge(hT_ready, i * 2 + k + 1)
                    for u in range(U):
                        ins = nc.tensor.matmul(pb[2 + 2 * k + u // 2][:, (u % 2) * 2 * P:(u % 2 + 1) * 2 * P], hT[:, k, :], w12[:, u, :],
                                               start=True, stop=True)
                    ins.then_inc(tab_ready, 1)
                if not last:
                    for k in range(2):
                        transpose_h(i + 1, k)
            for k in range(2):
                transpose_h(0, k)
            rounds_of(pe, NG // 2, tables)
            pe.wait_ge(t2s_ready, NG)

            nc.tensor.transpose(pb[7][0:HID, 0:ACC], wf2e[:, :], ident[0:ACC, 0:ACC]).then_inc(wf2T_ps, 1)
            pe.wait_ge(wf2T_ready, 1)
            nc.tensor.matmul(pb[7][0:ACC, 0:HID], wf2T[:, :], wn1[:, :], start=True, stop=True).then_inc(wflow_ps, 1)
            pe.wait_ge(wflow_ready, 1)

            for n, k in enumerate((1, 0)):
                pe.wait_ge(cnt_ready, n + 1)
                nc.tensor.matmul(pb[3][0:NB, 0:1], cum[:, k, 0:NB], ones[0:NP, 0:1], start=True, stop=True)
                nc.tensor.matmul(pb[3][0:NB, 1:2], cum[:, k, 1:NB + 1], ones[0:NP, 0:1], start=True, stop=True).then_inc(n_ready, 1)
                pe.wait_ge(tiles_ready, n + 1)
                nc.tensor.matmul(pb[3][0:NB, 2:3], upto[0:NB, 0:NB], tile_col[:, 3:4], start=True, stop=True).then_inc(tend_ready, 1)
                pe.wait_ge(ge_ready, n + 1)
                for c in range(J // JC):
                    w = n * (J // JC) + c
                    if w > 1:
                        pe.wait_ge(sched_read, w - 1)
                    cols = ge[:, c * JC:(c + 1) * JC]
                    nc.tensor.matmul(pb[sched_bank[w % 2]][:, 0:JC], c128[:, :], cols, start=True, stop=True)
                    nc.tensor.matmul(pb[sched_bank[w % 2] + 1][0:1, 0:JC], slack_h[:, k:k + 1], cols, start=True, stop=True).then_inc(sched_ps, 1)
                if k == 1:
                    nc.tensor.matmul(pb[7][0:NP, 0:NB], ones[0:NP, 0:NP], cum[:, 1, 0:NB], start=True, stop=False)
                    nc.tensor.matmul(pb[7][0:NP, 0:NB], before[0:NP, 0:NP], cnt[:, :], start=False, stop=True).then_inc(fbase_ps, 1)
                    pe.wait_ge(viol_ready, 1)
                    pe.wait_ge(fbase_ready, 1)
                    nc.tensor.matmul(pb[7][0:1, 256:257], viol[:, 2:3], ones[0:NP, 0:1], start=True, stop=True).then_inc(flag_ps, 1)

            pe.wait_ge(flag_ready, 1)
            nc.tensor.matmul(pb[7][:, 0:NB], ones[0:NP, :], cum[:, 0, 0:NB], start=True, stop=True).then_inc(begin_ps, 1)
            q = pb[4][:, 0:(U + 1) * NB].rearrange("p (u b) -> p u b", b=NB)

            def transposes(i, r, very_first=False):
                v = i * R + r + 1
                if not very_first:
                    pe.wait_ge(oht_ready, v - 1)
                    pe.sem_inc(pe_tick, 1)
                pe.wait_ge(ohd_ready, v)
                for u in range(U):
                    nc.tensor.transpose(pb[0][:, u * P:(u + 1) * P], ohd[:, r % 2, u, :], ident[:, :])
                pe.wait_ge(ld_ea[r], 16 * U * (i + 1))
                for u in range(U):
                    ins = nc.tensor.transpose(pb[1][0:EA + 1, u * P:(u + 1) * P], eat[:, r, u, :], ident[:, :])
                ins.then_inc(tp_ready, 1)

            def hidden(i, r):
                v = i * R + r + 1
                at = four(pe, blk[1], i * W + r * U, NB)
                pe.wait_ge(gat[r], 16 * U * (i + 1))
                pe.sem_inc(pe_tick, 1)
                pe.wait_ge(oht_ready, v)
                for u in range(U):
                    p = pb[2][:, u * P:(u + 1) * P]
                    nc.tensor.matmul(p, ident[:, :], g2[:, r, u, :], start=True, stop=False)
                    nc.tensor.matmul(p, eaT[:, r % 2, u, :], wee[:, :], start=False, stop=False)
                    ins = nc.tensor.matmul(p, oht[:, r % 2, u, :], t1[:, bass.ds(at[u], 1), :].rearrange("p a c -> p (a c)"), start=False, stop=True)
                ins.then_inc(pre_ready, 1)

            def counts(i, r, first):
                v = i * R + r + 1
                o = ohs[:, r % 2, :, :]
                if not (first and r == 0):
                    pe.wait_ge(q_read, v - 1)
                    pe.sem_inc(pe_tick, 1)
                pe.wait_ge(ohs_ready, v)
                nc.tensor.matmul(q[:, 0:U, :], before_h[:, :], o, start=True, stop=False)
                nc.tensor.matmul(q[:, U, :], ones_h[:, :], o[:, 0, :], start=False, stop=False)
                nc.tensor.matmul(q[:, 1:U, :], ones_h[:, :], bcast_mid(o[:, 0, :], U - 1), start=False, stop=False)
                for c in range(1, U):
                    ins = nc.tensor.matmul(q[:, c + 1:U + 1, :], ones_h[:, :], bcast_mid(o[:, c, :], U - c), start=False, stop=c == U - 1)
                ins.then_inc(q_ready, 1)

            def sums(i, r, first):
                v = i * R + r + 1
                if not (first and r == 0):
                    pe.wait_ge(acc_done, v - 1)
                    pe.sem_inc(pe_tick, 1)
                pe.wait_ge(relu_ready, v)
                for u in range(U):
                    ins = nc.tensor.matmul(pb[3][:, u * ACC:(u + 1) * ACC], ohd[:, r % 2, u, :], rf[:, u, :], start=True, stop=True)
                ins.then_inc(sum_ready, 1)

            def edges(i, first, last):
                for r in range(R):
                    hidden(i, r)
                    if r < R - 1:
                        transposes(i, r + 1)
                    elif not last:
                        transposes(i + 1, 0)
                    counts(i, r, first)
                    sums(i, r, first)
            transposes(0, 0, True)
            rounds(pe, edges)

            def sum_records(i, first, last):
                for w in range(SW):
                    at = window_of(pe, e0[0], (i * SW + w) * W, W - 1)
                    for r in range(R):
                        v = (i * SW + w) * R + r + 1
                        pe.wait_ge(soh_ready, v)
                        pe.sem_inc(pe_tick, 1)
                        for u in range(U):
                            ins = nc.tensor.matmul(s_bank[r][:, u * ACC:(u + 1) * ACC], s_oh[r][:, u, :],
                                                   srec[w][:, bass.ds(at[r * U + u], 1), 0:ACC].rearrange("p a c -> p (a c)"), start=True, stop=True)
                        ins.then_inc(ssum_ready, 1)
            pe.wait_ge(relu_ready, NI * R)
            pe.wait_ge(acc_done, NI * R)
            rounds_of(pe, NI // SW, sum_records)

            nc.tensor.matmul(pb[7][:, 0:D], ones[0:1, :], bn2r[:, :], start=True, stop=True).then_inc(b1_ready, 1)

            def transpose_sums(i, k, first):
                if not first:
                    pe.wait_ge(accT_ready, i * 2 + k - 1)
                    pe.sem_inc(pe_tick, 1)
                pe.wait_ge(accs_ready, i * 2 + k + 1)
                for u in range(U):
                    ins = nc.tensor.transpose(pb[k][0:ACC, u * P:(u + 1) * P], accs[:, k, u, :], ident[:, :])
                ins.then_inc(accT_ps, 1)

            def nodes(i, first, last):
                for k in range(2):
                    if not first:
                        pe.wait_ge(node_ready, i * 2 + k - 1)
                        pe.sem_inc(pe_tick, 1)
                    pe.wait_ge(accT_ready, i * 2 + k + 1)
                    pe.sem_inc(pe_tick, 1)
                    nc.tensor.matmul(pb[2 + k][0:HID, :], wflow[:, :], accT[:, k, :], start=True, stop=True).then_inc(node_ps, 1)
                if not last:
                    for k in range(2):
                        transpose_sums(i + 1, k, False)
                for k in range(2):
                    if not first:
                        pe.wait_ge(x1_done, i * 2 + k - 1)
                        pe.sem_inc(pe_tick, 1)
                    pe.wait_ge(node_ready, i * 2 + k + 1)
                    for u in range(U):
                        ins = nc.tensor.matmul(pb[5 + k][:, u * D:(u + 1) * D], nodeT[:, k, u * P:(u + 1) * P], wn2[:, :], start=True, stop=True)
                    ins.then_inc(outp_ps, 1)
            for k in range(2):
                transpose_sums(0, k, True)
            rounds_of(pe, NG // 2, nodes)

            def sum_neighbours(i, first, last):
                for r in range(R):
                    v = i * R + r + 1
                    if not (first and r < 2):
                        pe.wait_ge(nacc_done, v - 2)
                        pe.sem_inc(pe_tick, 1)
                    pe.wait_ge(gh[r], 16 * U * (i + 1))
                    pe.sem_inc(pe_tick, 1)
                    pe.wait_ge(noh_ready, v)
                    for u in range(U):
                        ins = nc.tensor.matmul(pb[5 + r % 2][:, u * D:(u + 1) * D], ohd[:, r % 2, u, :], h2g[:, r, u, :],
                                               start=True, stop=True)
                    ins.then_inc(nsum_ready, 1)
            rounds(pe, sum_neighbours)

        @block.vector
        def _(dve):
            own = Chain(dve, dve_own)

            def norm_relu(src, var_sem, std_sem):
                own.step(nc.vector.reduce_sum(stat[:, 0, :], src[:, :, :], axis=AX))
                own.step(nc.vector.tensor_scalar(stat[:, 0, :], stat[:, 0, :], 1.0 / D, None, ALU.mult))
                own.step(nc.vector.tensor_tensor(h[:, :, :], src[:, :, :], bcast(stat[:, 0, :], D), ALU.subtract))
                own.step(nc.vector.tensor_tensor(lnt[:, :, :], h[:, :, :], h[:, :, :], ALU.mult))
                own.step(nc.vector.reduce_sum(stat[:, 1, :], lnt[:, :, :], axis=AX))
                nc.vector.tensor_scalar(stat[:, 1, :], stat[:, 1, :], 1.0 / D, 1e-5, ALU.mult, ALU.add).then_inc(var_sem, 1)
                dve.wait_ge(std_sem, 1)
                own.step(nc.vector.reciprocal(stat[:, 0, :], stat[:, 1, :]))
                own.step(nc.vector.tensor_tensor(h[:, :, :], h[:, :, :], bcast(stat[:, 0, :], D), ALU.mult))
                return nc.vector.tensor_scalar(h[:, :, :], h[:, :, :], 0.0, None, ALU.max)

            dve.wait_ge(x_in, 32)
            norm_relu(xs, var_ready, std_ready).then_inc(h_ready, 1)

            dve.wait_ge(h_ready, 1)
            dve.wait_ge(nat_in, 32)
            dve.wait_ge(consts, 1)
            for k in (1, 0):
                own.step(nc.vector.tensor_scalar(blk_i, nat[:, :, k], 7, None, ALU.arith_shift_right))
                own.step(nc.vector.tensor_copy(nblk[:, k, :], blk_i))
            nc.vector.tensor_scalar(half_blk[:, :], iota_blk1[0:NP, 0:N_ACT], 0.5, None, ALU.subtract).then_inc(nblk_ready, 1)
            own.link(nc.vector.memset(row_nextf[:, :], float(FAR)))
            own.step(nc.vector.tensor_scalar(row_nexti[0:NP - 1, :], row_next[0:NP - 1, 1:2], 7, None, ALU.arith_shift_right))
            own.step(nc.vector.tensor_copy(row_nextf[0:NP - 1, :], row_nexti[0:NP - 1, :]))
            own.step(nc.vector.tensor_tensor(junk_d[:, 0:NC - 1], nblk[:, 1, 1:NC], nblk[:, 1, 0:NC - 1], ALU.is_lt))
            own.step(nc.vector.reduce_sum(viol[:, 0:1], junk_d[:, 0:NC - 1], axis=AX))
            own.step(nc.vector.tensor_tensor(viol[:, 1:2], row_nextf[:, :], nblk[:, 1, NC - 1:NC], ALU.is_lt))
            nc.vector.tensor_tensor(viol[:, 2:3], viol[:, 0:1], viol[:, 1:2], ALU.add).then_inc(viol_ready, 1)

            def count(k, b0, b1, before_):
                def one(b, m, first):
                    if not first:
                        dve.wait_ge(cum_ready, b + (before_ - b0 - 1))
                    nc.vector.tensor_scalar(junk_of["dve"][m], nblk[:, k, :], iota_blk1[0:NP, bass.ds(b, 1)], 0.0, ALU.is_lt, ALU.add,
                                            accum_out=cum[:, k, bass.ds(b + 1, 1)]).then_inc(cum_ready, 1)
                for m in range(2):
                    one(b0 + m, m, True)
                with dve.Fori(1, (b1 - b0) // 2) as i:
                    for m in range(2):
                        one(i * 2 + b0 + m, m, False)
                dve.wait_ge(cum_ready, before_ + b1 - b0)

            for n, k in enumerate((1, 0)):
                if k == 1:
                    count(k, 0, NB, 0)
                    nc.vector.tensor_tensor(cnt[:, :], cum[:, 1, 1:NB + 1], cum[:, 1, 0:NB], ALU.subtract).then_inc(cnt_ready, 1)
                else:
                    count(k, N_ACT, NB, NB)
                    dve.wait_ge(cum_act, N_ACT)
                    c = cum[:, 0, 1:N_ACT + 1]
                    nc.vector.tensor_scalar(c, c, 0.5, NC / 2, ALU.mult, ALU.add).then_inc(cnt_ready, 1)
                dve.wait_ge(n_ready, n + 1)
                own.step(nc.vector.tensor_copy(edge_col[:, 0:2], pb[3][0:NB, 0:2]))
                own.link(nc.vector.tensor_scalar(edge_col[:, 2:3], edge_col[:, 1:2], float(P - 1), None, ALU.add))
                own.link(nc.vector.tensor_tensor(edge_col[:, 3:4], edge_col[:, 1:2], edge_col[:, 0:1], ALU.is_gt))
                own.wait()
                own.step(nc.vector.tensor_copy(edge_coli[:, :], edge_col[:, 0:3]))
                own.step(nc.vector.tensor_scalar(edge_coli[:, :], edge_coli[:, :], 7, None, ALU.arith_shift_right))
                own.step(nc.vector.tensor_copy(tile_col[:, 0:3], edge_coli[:, :]))
                own.step(nc.vector.tensor_tensor(tile_col[:, 3:4], tile_col[:, 2:3], tile_col[:, 0:1], ALU.subtract))
                nc.vector.tensor_tensor(tile_col[:, 3:4], tile_col[:, 3:4], edge_col[:, 3:4], ALU.mult).then_inc(tiles_ready, 1)
                dve.wait_ge(tiles_ready, n + 1)
                own.step(nc.vector.tensor_tensor(slack[:, k:k + 1], tile_col[:, 1:2], tile_col[:, 0:1], ALU.subtract))
                own.step(nc.vector.tensor_tensor(slack[:, k:k + 1], slack[:, k:k + 1], tile_col[:, 3:4], ALU.subtract))
                own.link(nc.vector.tensor_scalar(slack_h[:, k:k + 1], slack[:, k:k + 1], float(P), None, ALU.mult))
                dve.wait_ge(tend_ready, n + 1)
                own.step(nc.vector.tensor_copy(tend[:, k:k + 1], pb[3][0:NB, 2:3]))
                nc.vector.tensor_scalar(ge[:, :], jrow[:, :], tend[:, k:k + 1], None, ALU.is_ge).then_inc(ge_ready, 1)
                for c in range(J // JC):
                    dve.wait_ge(sched_ps, n * (J // JC) + c + 1)
                    s = slice(c * JC, (c + 1) * JC)
                    bank = sched_bank[(n * (J // JC) + c) % 2]
                    nc.vector.tensor_copy(base_row[k][:, s], pb[bank][:, 0:JC])
                    nc.vector.tensor_scalar(blk[k][:, s], pb[bank][0:1, 0:JC], 1.0 / P, None, ALU.mult)
                    nc.vector.tensor_copy(e0f[:, s], pb[bank + 1][0:1, 0:JC]).then_inc(sched_read, 1)
                dve.wait_ge(sched_read, (n + 1) * (J // JC))
                own.step(nc.vector.scalar_tensor_tensor(e0f[:, :], jrow[0:1, :], float(P), e0f[:, :], op0=ALU.mult, op1=ALU.add))
                top = float(EP - W * P)
                if k == 1:
                    nc.vector.tensor_scalar(e0[k][:, :], e0f[:, :], top, None, ALU.min).then_inc(sched_done, 1)
                else:
                    own.step(nc.vector.tensor_scalar(e0f[:, :], e0f[:, :], top, None, ALU.min))
                    steps = e0f.rearrange("p (i s) -> p i s", s=W)
                    first_ = steps[:, :, 0]
                    own.link(nc.vector.tensor_copy(window[:, :], first_))
                    own.step(nc.vector.tensor_tensor(steps[:, :, 1:W], steps[:, :, 1:W], bcast(first_, W - 1), ALU.subtract))
                    own.step(nc.vector.tensor_scalar(steps[:, :, 0:1], steps[:, :, 0:1], 0.0, None, ALU.mult))
                    nc.vector.tensor_scalar(e0[k][:, :], e0f[:, :], 1.0 / P, None, ALU.mult).then_inc(sched_done, 1)
                if k == 1:
                    dve.wait_ge(fbase_ps, 1)
                    nc.vector.tensor_copy(fb_base, pb[7][0:NP, 0:NB]).then_inc(fbase_ready, 1)
                    dve.wait_ge(flag_ps, 1)
                    nc.vector.tensor_copy(flag[:, :], pb[7][0:1, 256:257]).then_inc(flag_ready, 1)
            dve.wait_ge(rearranged, 1)
            dve.wait_ge(sched_read, 2 * (J // JC))
            own.step(nc.vector.memset(acc[:, :, :], 0.0))
            dve.wait_ge(sched_done, 2)

            dve.wait_ge(begin_ps, 1)
            own.step(nc.vector.tensor_copy(q_row[:, 0, :], pb[7][:, 0:NB]))

            chain = Chain(dve, dve_d)
            q = pb[4][:, 0:(U + 1) * NB].rearrange("p (u b) -> p u b", b=NB)

            def small_of(r):
                return [small[:, r % 2, m, :] for m in range(7)]

            def dst_row(i, r):
                dloc = small_of(r)[0]
                dve.wait_ge(ld_sd[r], 16 * U * (i + 1))
                floats = chain.link(nc.vector.tensor_copy(sdf[:, r % 2, :, :], rec_i[:, r, :, :]))
                blocks = chain.link(nc.vector.tensor_scalar(sblk[:, r % 2, :], rec_i[:, r, :, 0], 7, None, ALU.arith_shift_right))
                chain.wait(floats)
                row = chain.link(nc.vector.tensor_tensor(dloc, sdf[:, r % 2, :, 1], base_row[1][:, bass.ds(i * W + r * U, U)], ALU.subtract))
                return row

            def dst_one_hot(r, row):
                dloc, clamp, valid, key, off, skey, _ = small_of(r)
                chain.wait(row)
                nc.vector.tensor_tensor(ohd[:, r % 2, :, :], bcast_mid(iota128[:, :], U), bcast(dloc, P), ALU.is_equal).then_inc(ohd_ready, 1)
                clamped = chain.link(nc.vector.tensor_scalar(clamp, dloc, 0.0, float(P - 1), ALU.max, ALU.min))
                chain.link(nc.vector.tensor_scalar(skey, sblk[:, r % 2, :], 1.0, None, ALU.add))
                return clamped

            def src_one_hot(r, clamped):
                dloc, clamp, valid, key, off, skey, _ = small_of(r)
                chain.wait(clamped)
                chain.step(nc.vector.tensor_tensor(valid, clamp, dloc, ALU.is_equal))
                keyed = chain.link(nc.vector.tensor_tensor(key, skey, valid, ALU.mult))
                chain.link(nc.vector.tensor_scalar(off, valid, -BIG, BIG, ALU.mult, ALU.add))
                chain.wait(keyed)
                nc.vector.tensor_tensor(ohs[:, r % 2, :, :], bcast_mid(iota_blk1[:, :], U), bcast(key, NB), ALU.is_equal).then_inc(ohs_ready, 1)

            def add_step(dst, at, src, width, u):
                to = dst[:, bass.ds(at[u], 1), :].rearrange("p a c -> p (a c)")
                return nc.vector.tensor_tensor(to, to, src[:, u * width:(u + 1) * width], ALU.add)

            def add_steps(dst, k, src, width, i, r, ready, done, links, first):
                v = i * R + r + 1
                at = four(dve, blk[k], i * W + r * U, NB)
                if not (first and r == 0):
                    dve.wait_ge(done, v - 1)
                    dve.sem_inc(dve_tick, 1)
                dve.wait_ge(ready, v)
                for u in range(U - 1):
                    links.step(add_step(dst, at, src, width, u))
                add_step(dst, at, src, width, U - 1).then_inc(done, 1)

            def positions(i, r, first):
                v = i * R + r + 1
                off, p = small_of(r)[4], small_of(r)[6]
                if not first:
                    dve.wait_ge(sct[r], 16 * U * i)
                    dve.sem_inc(dve_tick, 1)
                dve.wait_ge(q_ready, v)
                placed = chain.link(nc.vector.tensor_tensor(prod[:, :, :], q[:, 0:U, :], bcast_mid(q_row[:, r % 2, :], U), ALU.add))
                nc.vector.tensor_tensor(q_row[:, (r + 1) % 2, :], q_row[:, r % 2, :], q[:, U, :], ALU.add).then_inc(q_read, 1)
                chain.wait(placed)
                chain.link(nc.vector.tensor_tensor(prod[:, :, :], prod[:, :, :], ohs[:, r % 2, :, :], ALU.mult))
                chain.wait()
                chain.step(nc.vector.reduce_sum(p, prod[:, :, :], axis=AX))
                nc.vector.tensor_tensor(pos[:, r, :], p, off, ALU.add).then_inc(pos_ready, 1)

            def add_and_prepare(i, r, first, ahead):
                v = i * R + r + 1
                at = four(dve, blk[1], i * W + r * U, NB)
                if not (first and r == 0):
                    dve.wait_ge(acc_done, v - 1)
                    dve.sem_inc(dve_tick, 1)
                dve.wait_ge(sum_ready, v)
                added = chain.link(add_step(acc, at, pb[3], ACC, 0))
                row = dst_row(*ahead) if ahead else None
                chain.wait(added)
                added = chain.link(add_step(acc, at, pb[3], ACC, 1))
                clamped = dst_one_hot(ahead[1], row) if ahead else None
                chain.wait(added)
                added = chain.link(add_step(acc, at, pb[3], ACC, 2))
                if ahead:
                    src_one_hot(ahead[1], clamped)
                chain.wait(added)
                add_step(acc, at, pb[3], ACC, 3).then_inc(acc_done, 1)

            assert U == 4
            per = R * (8 + 3 + 3)

            def edges(i, first, last):
                chain.n, chain.base = FRONT, i * per
                for r in range(R):
                    positions(i, r, first)
                    ahead = (i, r + 2) if r < R - 2 else None if last else (i + 1, r + 2 - R)
                    add_and_prepare(i, r, first, ahead)
                assert last or chain.n == FRONT + per, (chain.n, FRONT, per)
            for r in range(2):
                src_one_hot(r, dst_one_hot(r, dst_row(0, r)))
            FRONT = chain.n
            assert FRONT == 16
            rounds(dve, edges)

            schain = Chain(dve, dve_s)
            dve.wait_ge(pre_ready, NI * R)
            AHEAD = R - 1

            def src_rows(i, w):
                cols = bass.ds((i * SW + w) * W, W)
                dve.wait_ge(pair_ready, (i * SW + w + 1) * R)
                dve.sem_inc(dve_tick, 1)
                return schain.link(nc.vector.tensor_tensor(pairs[:, cols, 0], pairs[:, cols, 0], base_row[0][:, cols], ALU.subtract))

            def src_row_one_hot(i, w, r, u):
                col = bass.ds((i * SW + w) * W + r * U + u, 1)
                ins = nc.vector.tensor_tensor(s_oh[r][:, u, :], iota128[:, :], pairs[:, col, 0].broadcast_to([P, P]), ALU.is_equal)
                if u == U - 1:
                    ins.then_inc(soh_ready, 1)

            per_s = SW * (R * 3 + 1)

            def records_summed(i, first, last):
                schain.n, schain.base = 1, i * per_s
                for w in range(SW):
                    at = window_of(dve, blk[0], (i * SW + w) * W, NB)
                    for r in range(R):
                        v = (i * SW + w) * R + r + 1
                        window = (i, w) if r < R - AHEAD else (i, w + 1) if w < SW - 1 else None if last else (i + 1, 0)
                        later = (r + AHEAD) % R
                        rows = src_rows(*window) if window and later == 0 else None
                        for u in range(U):
                            if u:
                                schain.wait(added)
                            else:
                                if not (first and w == 0 and r == 0):
                                    dve.wait_ge(sacc_done, v - 1)
                                    dve.sem_inc(dve_tick, 1)
                                dve.wait_ge(ssum_ready, v)
                            ins = add_step(acc, at[r * U:(r + 1) * U], s_bank[r], ACC, u)
                            if u < U - 1:
                                added = schain.link(ins)
                            else:
                                ins.then_inc(sacc_done, 1)
                            if window:
                                if u == 0 and rows is not None:
                                    schain.wait(rows)
                                src_row_one_hot(*window, later, u)
                assert last or schain.n == 1 + per_s
            schain.wait(src_rows(0, 0))
            for r in range(AHEAD):
                for u in range(U):
                    src_row_one_hot(0, 0, r, u)
            rounds_of(dve, NI // SW, records_summed)

            dve.wait_ge(b1_ready, 1)
            own.step(nc.vector.tensor_copy(bn2b[:, :], pb[7][:, 0:D]))
            own.step(nc.vector.tensor_tensor(xs[:, :, :], xs[:, :, :], bcast_mid(bn2b[:, :], NBP), ALU.add))

            def nodes(i, first, last):
                for k in range(2):
                    dve.wait_ge(outp_ps, i * 2 + k + 1)
                    to = xs[:, bass.ds((i * 2 + k) * U, U), :]
                    nc.vector.tensor_tensor(to, to, pb[5 + k][:, 0:U * D].rearrange("p (u f) -> p u f", u=U), ALU.add).then_inc(x1_done, 1)
            rounds_of(dve, NG // 2, nodes)
            dve.wait_ge(x1_done, NG)
            norm_relu(xs, var2_ready, std2_ready).then_inc(h2_ready, 1)

            gchain = Chain(dve, dve_g)
            dve.wait_ge(acc2_zero, 1)

            def neighbour_one_hots(i, r):
                cols = bass.ds(i * W + r * U, U)
                nc.vector.tensor_tensor(ohd[:, r % 2, :, :], bcast_mid(iota128[:, :], U), bcast(pairs[:, cols, 0], P), ALU.is_equal).then_inc(noh_ready, 1)

            def neighbours(i, first, last):
                gchain.n, gchain.base = 0, i * R * 3
                for r in range(R):
                    if r < R - 1:
                        neighbour_one_hots(i, r + 1)
                    elif not last:
                        neighbour_one_hots(i + 1, 0)
                    add_steps(acc2, 0, pb[5 + r % 2], D, i, r, nsum_ready, nacc_done, gchain, first)
            neighbour_one_hots(0, 0)
            rounds(dve, neighbours)
            dve.wait_ge(nacc_done, NI * R)
            nc.vector.tensor_tensor(lnt[:, :, :], xs[:, :, :], acc2[:, :, :], ALU.add).then_inc(y_ready, 1)


N_W = 16 + 4 + 6


def kernel(**inputs):
    import numpy as np
    import concourse.bacc as bacc
    from concourse.bass_utils import run_bass_kernel_spmd

    nc = bacc.Bacc("TRN2", target_bir_lowering=False, num_devices=1)
    laid = {"x": inputs["x"], "sd": np.stack([inputs["src"], inputs["dst"]], axis=1), "ea": inputs["edge_attr_16"]}
    for name in ("Wf1", "bf1", "Wf2", "bf2", "Wn1", "bn1", "Wn2", "bn2"):
        laid[name] = inputs[f"L0_gnn_{name}"]
    arrays, args = {}, []
    for name, a in laid.items():
        a = np.ascontiguousarray(a)
        arrays[f"in_{name}"] = a
        args.append(nc.dram_tensor(f"in_{name}", a.shape, mybir.dt.from_np(a.dtype), kind="ExternalInput").ap())
    args.append(nc.dram_tensor("out_x", (N, D), F32, kind="ExternalOutput").ap())
    build(nc, *args)
    r = run_bass_kernel_spmd(nc, [arrays], core_ids=[0])
    return r.results[0]["out_x"]
```

```python
from contextlib import ExitStack

import concourse.bass as bass
from concourse import mybir

P = 128
F32 = mybir.dt.float32
BF16 = mybir.dt.bfloat16
I32 = mybir.dt.int32
U32 = mybir.dt.uint32
ALU = mybir.AluOpType
ACT = mybir.ActivationFunctionType
AX = mybir.AxisListType.X

N, D, E, EA, HID = 12500, 32, 200000, 16, 64
NB = -(-N // P)
U = 4
R = 4
NBP = -(-(NB + 1) // (2 * U)) * 2 * U
NG = NBP // U
W = U * R
NI = -(-(-(-E // P) + NB) // W)
J = NI * W
EP = (-(-E // P) + W) * P
NP, NC = 125, E // 125
REC = HID + 3
ACC = HID + 1
FAR = 32768
BIG = float(1 << 22)
JC = J // 4
N_ACT = 46
SW = 4
TW = -(-(-(-E // P)) // W)
RING = 16
assert E % 125 == 0 and JC <= 512 and J % 4 == 0 and NI % SW == 0 and TW < NI - SW and EP >= TW * W * P and EP // P - W < TW * W


class Chain:

    def __init__(self, eng, sem, tick=None):
        self.eng, self.sem, self.n, self.base, self.tick = eng, sem, 0, 0, tick

    def link(self, ins):
        self.n += 1
        ins.then_inc(self.sem, 1)
        return self.n

    def wait(self, mark=None):
        self.eng.wait_ge(self.sem, self.base + (self.n if mark is None else mark))
        if self.tick is not None:
            self.eng.sem_inc(self.tick, 1)

    def step(self, ins):
        self.link(ins)
        self.wait()


def bcast(ap, n):
    return ap.unsqueeze(2).broadcast_to([ap.shape[0], ap.shape[1], n])


def bcast_mid(ap, n):
    return ap.unsqueeze(1).broadcast_to([ap.shape[0], n, ap.shape[1]])


def build(nc, x, sd, ea, Wf1, bf1, Wf2, bf2, Wn1, bn1, Wn2, bn2, out):
    with ExitStack() as ctx:
        def sb(name, shape, dt=F32):
            return ctx.enter_context(nc.sbuf_tensor(name, shape, dt))

        def sem(name):
            return ctx.enter_context(nc.semaphore(name))

        def sems(name, n):
            return [sem(f"{name}{i}") for i in range(n)]

        def dram(name, shape, dt=F32):
            return nc.dram_tensor(name, shape, dt).ap()

        by_d_sd = dram("by_d_sd", [EP, 2], I32)
        by_d_ea = dram("by_d_ea", [EP, EA])
        t2_rows = dram("t2_rows", [NBP * P, P])
        records = dram("records", [EP, REC])
        h2_rows = dram("h2_rows", [NBP * P, D])

        iota128 = sb("iota128", [P, P])
        iota_blk1 = sb("iota_blk1", [P, NB])
        ones = sb("ones", [P, P])
        ident = sb("ident", [P, P])
        before = sb("before", [P, P])
        upto = sb("upto", [P, P])
        ones_h = sb("ones_h", [P, P], BF16)
        before_h = sb("before_h", [P, P], BF16)
        tail_sd = sb("tail_sd", [P, 2], I32)
        tail_rec = sb("tail_rec", [P, REC])
        w12 = sb("w12", [P, U, 2 * P])
        wee = sb("wee", [EA + 1, P])
        wf2e = sb("wf2e", [ACC, HID])
        wf2T = sb("wf2T", [HID, ACC])
        wflow = sb("wflow", [ACC, 2, 2 * HID])
        wn1 = sb("wn1", [HID, HID])
        bn1c = sb("bn1c", [2 * HID, 1])
        wn2 = sb("wn2", [2 * HID, 2, D])
        bn2r = sb("bn2r", [1, D])
        xs = sb("xs", [P, NBP, D])
        h = sb("h", [P, NBP, D])
        lnt = sb("lnt", [P, NBP, D])
        stat = sb("stat", [P, 2, NBP])
        t1 = sb("t1", [P, NBP, P])
        acc = sb("acc", [P, NBP, ACC])
        acc_flat = acc[:, :, :].rearrange("p b c -> p (b c)")
        jrow = acc_flat[0:NB, 0:J]
        ge = acc_flat[0:NB, J:J + J // 2].bitcast(BF16)
        nblk = acc_flat[0:NP, 2 * J:2 * J + NC].bitcast(BF16).rearrange("p (k c) -> p k c", k=2)
        assert 2 * J + NC <= NBP * ACC
        acc2 = t1[:, 0:NG, :].rearrange("p b (u f) -> p (b u) f", f=D)
        t1_rest = t1[:, NG:NBP, :].rearrange("p b c -> p (b c)")
        srec = [t1_rest[:, w * W * REC:(w + 1) * W * REC].rearrange("p (t c) -> p t c", c=REC) for w in range(SW)]
        at_ = SW * W * REC
        accs = t1_rest[:, at_:at_ + 2 * U * ACC].rearrange("p (k u c) -> p k u c", k=2, u=U)
        at_ += 2 * U * ACC
        accT = t1_rest[0:ACC, at_:at_ + 2 * U * P].rearrange("p (k n) -> p k n", k=2)
        at_ += 2 * U * P
        nodeT = t1_rest[0:2 * HID, at_:at_ + U * P]
        at_ += U * P
        assert at_ <= (NBP - NG) * P
        hs = sb("hs", [P, 2, P])
        hT = sb("hT", [P, 2, P])
        t2s = sb("t2s", [P, 2, U, P])
        raw = sb("raw", [P, 2, J], I32)
        nat = raw[:, :, :].rearrange("p k j -> p (k j)")[0:NP, 0:2 * NC].rearrange("p (c k) -> p c k", k=2)
        pairs = raw[:, :, :].rearrange("p k j -> p (k j)").bitcast(F32).rearrange("p (j k) -> p j k", k=2)
        wide = sb("wide", [P, 2, J])
        base_row = [wide[:, k, :] for k in range(2)]
        blk_i = lnt[0:NP, 0:NC // D, :].rearrange("p b f -> p (b f)").bitcast(I32)
        assert NC % D == 0
        e0f = lnt[0:1, 0:J // D, :].rearrange("p b f -> p (b f)")
        junk_d = sb("junk_d", [NP, NC], BF16)
        half_blk = sb("half_blk", [NP, N_ACT])
        row_next = sb("row_next", [NP, 2], I32)
        row_nexti = sb("row_nexti", [NP, 1], I32)
        row_nextf = sb("row_nextf", [NP, 1])
        viol = sb("viol", [NP, 3])
        flag = sb("flag", [1, 1], I32)
        cum = sb("cum", [NP, 2, NB + 1])
        cnt = sb("cnt", [NP, NB])
        edge_col = sb("edge_col", [NB, 4])
        edge_coli = sb("edge_coli", [NB, 3], I32)
        tile_col = sb("tile_col", [NB, 4])
        tend = sb("tend", [NB, 2])
        slack = sb("slack", [NB, 2])
        slack_h = sb("slack_h", [NB, 2], BF16)
        c128 = sb("c128", [NB, P], BF16)
        sched = sb("sched", [P, J], I32)
        e0 = [sched[32 * k:32 * k + 1, :] for k in (0, 1)]
        window = sb("window", [1, NI], I32)
        window_f = sb("window_f", [1, NI])
        blk = [sched[32 * k:32 * k + 1, :] for k in (2, 3)]
        rec = sb("rec", [P, R, U, REC])
        rec_i = sb("rec_i", [P, R, U, 2], I32)
        eat = sb("eat", [P, R, U, EA + 1])
        g2 = sb("g2", [P, R, U, P])
        sdf = sb("sdf", [P, 2, U, 2])
        small = sb("small", [P, 2, 7, U])
        sblk = sb("sblk", [P, 2, U], I32)
        ohd = sb("ohd", [P, 2, U, P])
        ohs = sb("ohs", [P, 2, U, NB], BF16)
        prod = sb("prod", [P, U, NB])
        pos = sb("pos", [P, R, U], I32)
        q_row = sb("q_row", [P, 2, NB])
        oht = sb("oht", [P, 2, U, P])
        eaT = sb("eaT", [EA + 1, 2, U, P])
        rf = sb("rf", [P, U, ACC])
        junk_of = {"dve": [junk_d[:, :], oht[:, :, :, :].rearrange("p k u n -> p (k u n)").bitcast(BF16)[0:NP, 0:NC]],
                   "act": [t[:, :, :, :].rearrange("p k u n -> p (k u n)").bitcast(BF16)[0:NP, 0:NC] for t in (ohd, g2)]}
        s_oh = [ohd[:, 0, :, :], ohd[:, 1, :, :], oht[:, 0, :, :], oht[:, 1, :, :]]
        didx = sb("didx", [P, SW, W, 2], I32)
        h2g = t1_rest[:, 0:RING * W * D].rearrange("p (t f) -> p t f", f=D)
        assert RING * W * D <= (NBP - NG) * P
        ring_slot = e0[1]
        bn2b = sb("bn2b", [P, D])

        fb_base = sb("fb_base", [NP, NB])[:, :]
        fb_blk = sb("fb_blk", [NP, 1])
        fb_oh = sb("fb_oh", [NP, NB])
        fb_prod = sb("fb_prod", [NP, P])
        fb_pos = sb("fb_pos", [NP, 1])
        fb_posi = sb("fb_posi", [NP, 1], I32)
        fb_sd = sb("fb_sd", [NP, 2], I32)
        fb_ea = sb("fb_ea", [NP, EA])
        fb_own = sem("fb_own")

        pb = [ctx.enter_context(nc.psum_tensor(f"bank{i}", [P, 512], F32)) for i in range(8)]

        x_in, w_in, nat_in = sem("x_in"), sem("w_in"), sem("nat_in")
        by_d_copied = sem("by_d_copied")
        tails_set = sem("tails_set")
        consts = sem("consts")
        pool_own, dve_own, act_own = sem("pool_own"), sem("dve_own"), sem("act_own")
        rearranged = sem("rearranged")
        var_ready, std_ready, h_ready = sem("var_ready"), sem("std_ready"), sem("h_ready")
        hs_ready, hsT_ready, hT_ready, tab_ready = sem("hs_ready"), sem("hsT_ready"), sem("hT_ready"), sem("tab_ready")
        t1_ready, t2s_ready, t2_written = sem("t1_ready"), sem("t2s_ready"), sems("t2_written", 2)
        b1_ready = sem("b1_ready")
        nblk_ready, cum_act = sem("nblk_ready"), sem("cum_act")
        cum_ready = sem("cum_ready")
        cnt_ready, n_ready, tiles_ready, tend_ready = sem("cnt_ready"), sem("n_ready"), sem("tiles_ready"), sem("tend_ready")
        ge_ready, sched_ps, sched_read, sched_done = sem("ge_ready"), sem("sched_ps"), sem("sched_read"), sem("sched_done")
        viol_ready, flag_ps, flag_ready = sem("viol_ready"), sem("flag_ps"), sem("flag_ready")
        begin_ps = sem("begin_ps")
        fbase_ps, fbase_ready = sem("fbase_ps"), sem("fbase_ready")
        fb_ld, fb_sc = sem("fb_ld"), sems("fb_sc", 2)
        ld_sd, ld_ea, gat, sct = sems("ld_sd", R), sems("ld_ea", R), sems("gat", R), sems("sct", R)
        ohd_ready, ohs_ready, tp_ready, oht_ready = sem("ohd_ready"), sem("ohs_ready"), sem("tp_ready"), sem("oht_ready")
        q_ready, q_read, pos_ready = sem("q_ready"), sem("q_read"), sem("pos_ready")
        pre_ready, relu_ready, sum_ready, acc_done = sem("pre_ready"), sem("relu_ready"), sem("sum_ready"), sem("acc_done")
        pool_tick, act_tick, pe_tick, dve_tick = sem("pool_tick"), sem("act_tick"), sem("pe_tick"), sem("dve_tick")
        dve_d = sem("dve_d")
        ld_srec = sems("ld_srec", SW)
        pair_ready, soh_ready, ssum_ready, dve_s = sem("pair_ready"), sem("soh_ready"), sem("ssum_ready"), sem("dve_s")
        accs_ready, accT_ps, accT_ready = sem("accs_ready"), sem("accT_ps"), sem("accT_ready")
        wf2T_ps, wf2T_ready, wflow_ps, wflow_ready = sem("wf2T_ps"), sem("wf2T_ready"), sem("wflow_ps"), sem("wflow_ready")
        node_ps, node_ready = sem("node_ps"), sem("node_ready")
        outp_ps, x1_done, dve_n = sem("outp_ps"), sem("x1_done"), sem("dve_n")
        var2_ready, std2_ready, h2_ready, h2_written = sem("var2_ready"), sem("std2_ready"), sem("h2_ready"), sem("h2_written")
        ld_didx, gh, slots_ready = sems("ld_didx", SW), sems("gh", SW), sem("slots_ready")
        noh_ready, nsum_ready, all_added, dve_g = sem("noh_ready"), sem("nsum_ready"), sem("all_added"), sem("dve_g")
        acc2_set, y_out = sem("acc2_set"), sem("y_out")

        sched_bank = [3, 5]
        s_bank = [pb[5], pb[6], pb[2], pb[3]]
        block = ctx.enter_context(nc.Block())
        N_FULL = N // P
        N_TAIL = N - N_FULL * P

        def four(eng, row, j0, top):
            return nc.values_load_multi_w_load_instructions(
                row[0:1, bass.ds(j0, U)], engines=[eng.engine], min_val=0, max_val=top,
                skip_runtime_bounds_check_because="the schedule clamps it to this range")[1]

        def window_of(eng, row, j0, top):
            return nc.values_load_multi_w_load_instructions(
                row[0:1, bass.ds(j0, W)], engines=[eng.engine], min_val=0, max_val=top,
                skip_runtime_bounds_check_because="the schedule clamps it to this range")[1]

        def rounds(eng, body):
            body(0, True, False)
            with eng.Fori(1, NI - 1) as i:
                body(i, False, False)
            body(NI - 1, False, True)

        def rounds_of(eng, n, body):
            body(0, True, False)
            with eng.Fori(1, n - 1) as i:
                body(i, False, False)
            body(n - 1, False, True)

        @block.sync
        def _(sp):
            sp.dma_start(nat[:, :, :], sd.rearrange("(p c) k -> p c k", p=NP)).then_inc(nat_in, 16)
            sp.dma_start(row_next[0:NP - 1, :], sd.rearrange("(p c) k -> p c k", p=NP)[1:NP, 0, :]).then_inc(nat_in, 16)
            sp.dma_start(xs[:, 0:N_FULL, :], x[0:N_FULL * P, :].rearrange("(b p) f -> p b f", p=P)).then_inc(x_in, 16)
            sp.wait_ge(tails_set, 1)
            sp.dma_start(xs[0:N_TAIL, N_FULL, :], x[N_FULL * P:N, :]).then_inc(x_in, 16)
            n_w = 0
            for u in range(U):
                for c, r0 in enumerate((0, D, D, 0)):
                    sp.dma_start(w12[u * D:(u + 1) * D, u, c * HID:(c + 1) * HID], Wf1[r0:r0 + D, :]).then_inc(w_in, 16)
                    n_w += 1
            for c in range(2):
                sp.dma_start(wee[0:EA, c * HID:(c + 1) * HID], Wf1[2 * D:2 * D + EA, :]).then_inc(w_in, 16)
                sp.dma_start(wee[EA:EA + 1, c * HID:(c + 1) * HID], bf1.unsqueeze(0)).then_inc(w_in, 16)
                n_w += 2
            for dst_, src_ in ((wf2e[0:HID, :], Wf2), (wf2e[HID:ACC, :], bf2.unsqueeze(0)), (wn1[:, :], Wn1),
                               (bn1c[0:HID, :], bn1.unsqueeze(1)), (bn1c[HID:2 * HID, :], bn1.unsqueeze(1)),
                               (wn2[0:HID, 0, :], Wn2), (wn2[HID:2 * HID, 1, :], Wn2), (bn2r[:, :], bn2.unsqueeze(0))):
                sp.dma_start(dst_, src_).then_inc(w_in, 16)
                n_w += 1
            assert n_w == N_W
            for to, of in ((by_d_sd, sd), (by_d_ea, ea)):
                sp.dma_start(to[0:E, :].rearrange("(p c) f -> p (c f)", p=1600),
                             of.rearrange("(p c) f -> p (c f)", p=1600)).then_inc(by_d_copied, 16)
            for to, of in ((by_d_sd, tail_sd[:, :]), (by_d_ea, tail_rec[:, 0:EA]), (records, tail_rec[:, :])):
                sp.dma_start(to[E:EP - W * P, :], of[0:EP - W * P - E, :]).then_inc(by_d_copied, 16)
                sp.dma_start(to[EP - W * P:EP, :].rearrange("(t p) f -> p t f", p=P), bcast_mid(of, W)).then_inc(by_d_copied, 16)

            def store_t2(i, first, last):
                for k in range(2):
                    sp.wait_ge(t2s_ready, i * 2 + k + 1)
                    sp.dma_start(t2_rows[bass.ds((i * 2 + k) * (U * P), U * P), :].rearrange("(u p) f -> p u f", p=P),
                                 t2s[:, k, :, :]).then_inc(t2_written[k], 16)
            rounds_of(sp, NG // 2, store_t2)

            sp.wait_ge(sched_done, 1)
            sp.wait_ge(rearranged, 1)

            def load_edges(i, first, last):
                for r in range(R):
                    at = four(sp, e0[1], i * W + r * U, EP - W * P)
                    if not first:
                        sp.wait_ge(relu_ready, i * R + r + 1 - R)
                    for u in range(U):
                        sp.dma_start(rec_i[:, r, u, :], by_d_sd[bass.ds(at[u], P), :]).then_inc(ld_sd[r], 16)
                    for u in range(U):
                        sp.dma_start(eat[:, r, u, 0:EA], by_d_ea[bass.ds(at[u], P), :]).then_inc(ld_ea[r], 16)
            rounds(sp, load_edges)

            sp.wait_ge(sched_done, 2)
            for r in range(R):
                sp.wait_ge(sct[r], 16 * U * NI)

            def load_records(i, first, last):
                for w in range(SW):
                    at = nc.values_load_multi_w_load_instructions(
                        window[0:1, bass.ds(i * SW + w, 1)], engines=[sp.engine], min_val=0, max_val=EP - W * P,
                        skip_runtime_bounds_check_because="the schedule clamps it to this range")[1][0]
                    if not first:
                        sp.wait_ge(ssum_ready, (i * SW + w + 1) * R - SW * R)
                    sp.dma_start(srec[w], records[bass.ds(at, W * P), :].rearrange("(t p) c -> p t c", p=P)).then_inc(ld_srec[w], 16)
            rounds_of(sp, NI // SW, load_records)

            sp.wait_ge(h2_ready, 1)
            sp.dma_start(h2_rows.rearrange("(b p) f -> p b f", p=P), h[:, :, :]).then_inc(h2_written, 16)

            def load_dst(i, first, windows=SW):
                for w in range(windows):
                    if not first:
                        sp.wait_ge(gh[w], 16 * W * i)
                    sp.dma_start(didx[:, w, :, :], records[bass.ds((i * SW + w) * (W * P), W * P), HID + 1:REC].bitcast(I32)
                                 .rearrange("(t p) c -> p t c", p=P)).then_inc(ld_didx[w], 16)
            load_dst(0, True)
            with sp.Fori(1, TW // SW) as i:
                load_dst(i, False)
            load_dst(TW // SW, False, TW % SW)

            sp.wait_ge(all_added, 1)
            sp.dma_start(out[0:N_FULL * P, :].rearrange("(b p) f -> p b f", p=P), acc2[:, 0:N_FULL, :]).then_inc(y_out, 16)
            sp.dma_start(out[N_FULL * P:N, :], acc2[0:N_TAIL, N_FULL, :]).then_inc(y_out, 16)
            sp.wait_ge(y_out, 32)
            sp.wait_ge(h2_written, 16)
            sp.wait_ge(by_d_copied, 16 * 8)
            for k in range(2):
                sp.wait_ge(t2_written[k], 16 * (NG // 2))

        FB_STEPS = 13

        def rearrange_edges(pool):
            ea_cols = ea.rearrange("(p c) f -> p c f", p=NP)
            last_row = pool.to_reg(E - 1)

            def column(c):
                own = Chain(pool, fb_own, pool_tick)
                own.base = c * FB_STEPS
                pool.dma_start(fb_ea[:, :], ea_cols[:, bass.ds(c, 1), :].rearrange("p a f -> p (a f)")).then_inc(fb_ld, 16)
                own.link(nc.gpsimd.tensor_copy(fb_blk[:, :], nblk[:, 1, bass.ds(c, 1)]))
                own.link(nc.gpsimd.tensor_copy(fb_sd[:, :], nat[:, bass.ds(c, 1), :].rearrange("p a k -> p (a k)")))
                own.wait()
                own.step(nc.gpsimd.tensor_scalar(fb_oh[:, :], iota128[0:NP, 0:NB], fb_blk[:, 0:1], None, ALU.is_equal))
                own.step(nc.gpsimd.tensor_tensor(fb_prod[:, 0:NB], fb_oh[:, :], fb_base, ALU.mult))
                for w in (64, 32, 16, 8, 4, 2):
                    own.step(nc.gpsimd.tensor_tensor(fb_prod[:, 0:w], fb_prod[:, 0:w], fb_prod[:, w:2 * w], ALU.add))
                own.link(nc.gpsimd.tensor_tensor(fb_pos[:, :], fb_prod[:, 0:1], fb_prod[:, 1:2], ALU.add))
                own.step(nc.gpsimd.tensor_tensor(fb_base, fb_base, fb_oh[:, :], ALU.add))
                own.link(nc.gpsimd.tensor_copy(fb_posi[:, :], fb_pos[:, :]))
                own.wait()
                assert own.n == FB_STEPS
                pool.wait_ge(fb_ld, 16 * (c + 1))
                pool.sem_inc(pool_tick, 1)
                for k, (rows, to) in enumerate(((fb_sd, by_d_sd), (fb_ea, by_d_ea))):
                    nc.gpsimd.indirect_dma_start(
                        out=to, out_offset=bass.IndirectOffsetOnAxis(ap=fb_posi[:, :].bitcast(U32), axis=0),
                        in_=rows[:, :], in_offset=None, bounds_check=last_row, oob_is_err=False).then_inc(fb_sc[k], 16)
                for k in range(2):
                    pool.wait_ge(fb_sc[k], 16 * (c + 1))
                    pool.sem_inc(pool_tick, 1)
            with pool.Fori(0, NC) as c:
                column(c)

        @block.gpsimd
        def _(pool):
            nc.gpsimd.memset(xs[:, N_FULL:NBP, :], 0.0)
            nc.gpsimd.memset(tail_rec[:, 0:HID + 1], 0.0)
            nc.gpsimd.memset(w12[:, :, :], 0.0)
            nc.gpsimd.memset(wn2[:, :, :], 0.0)
            nc.gpsimd.memset(wflow[:, :, :], 0.0)
            nc.gpsimd.memset(fb_prod[:, :], 0.0)
            nc.gpsimd.memset(tail_sd[:, 0:1], 0)
            nc.gpsimd.memset(tail_sd[:, 1:2], FAR)
            nc.gpsimd.memset(tail_rec[:, HID + 1:HID + 2].bitcast(I32), FAR)
            nc.gpsimd.memset(tail_rec[:, HID + 2:HID + 3].bitcast(I32), 0).then_inc(tails_set, 1)
            own = Chain(pool, pool_own)
            nc.gpsimd.iota(iota128[:, :], [[1, P]], base=0, channel_multiplier=0, allow_small_or_imprecise_dtypes=True)
            nc.gpsimd.iota(iota_blk1[:, :], [[1, NB]], base=1, channel_multiplier=0, allow_small_or_imprecise_dtypes=True)
            nc.gpsimd.iota(jrow[:, :], [[1, J]], base=0, channel_multiplier=0, allow_small_or_imprecise_dtypes=True)
            nc.gpsimd.memset(ones[:, :], 1.0)
            nc.gpsimd.memset(ones_h[:, :], 1.0)
            nc.gpsimd.memset(c128[:, :], float(P))
            nc.gpsimd.memset(cum[:, :, 0:1], 0.0)
            nc.gpsimd.memset(rf[:, :, HID:ACC], 1.0)
            nc.gpsimd.memset(rec[:, :, :, HID:HID + 1], 1.0)
            own.step(nc.gpsimd.memset(eat[:, :, :, EA:EA + 1], 1.0))
            for m, op in ((before, ALU.is_gt), (upto, ALU.is_ge), (ident, ALU.is_equal), (before_h, ALU.is_gt)):
                ins = nc.gpsimd.affine_select(out=m[:, :], in_=ones[:, :], compare_op=op, fill=0.0, base=0,
                                              pattern=[[1, P]], channel_multiplier=-1)
            ins.then_inc(consts, 1)

            pool.wait_ge(by_d_copied, 16 * 8)
            pool.wait_ge(flag_ready, 1)
            pool.wait_ge(fbase_ready, 1)
            unsorted_edges = pool.value_load(flag[0:1, 0:1], min_val=0, max_val=1 << 20)
            with pool.If(unsorted_edges > 0):
                rearrange_edges(pool)
            with pool.Else():
                pool.sem_inc(pool_tick, 1)
            pool.sem_inc(rearranged, 1)

            for k in range(2):
                pool.wait_ge(t2_written[k], 16 * (NG // 2))
            pool.wait_ge(cum_act, N_ACT)
            end = pool.to_reg(E - 1)

            def gather_t2(i, r):
                pool.wait_ge(ld_sd[r], 16 * U * (i + 1))
                pool.sem_inc(pool_tick, 1)
                for u in range(U):
                    nc.gpsimd.indirect_dma_start(
                        out=g2[:, r, u, :], out_offset=None, in_=t2_rows,
                        in_offset=bass.IndirectOffsetOnAxis(ap=rec_i[:, r, u, 0:1].bitcast(U32), axis=0)).then_inc(gat[r], 16)

            def scatter_records(i, r):
                pool.wait_ge(pos_ready, i * R + r + 1)
                pool.sem_inc(pool_tick, 1)
                pool.wait_ge(relu_ready, i * R + r + 1)
                pool.sem_inc(pool_tick, 1)
                for u in range(U):
                    nc.gpsimd.indirect_dma_start(
                        out=records, out_offset=bass.IndirectOffsetOnAxis(ap=pos[:, r, u:u + 1].bitcast(U32), axis=0),
                        in_=rec[:, r, u, :], in_offset=None, bounds_check=end, oob_is_err=False).then_inc(sct[r], 16)

            def edges(i, first, last):
                for r in range(R):
                    if r < R - 2:
                        gather_t2(i, r + 2)
                    elif not last:
                        gather_t2(i + 1, r + 2 - R)
                    scatter_records(i, r)
            gather_t2(0, 0)
            gather_t2(0, 1)
            rounds(pool, edges)

            pool.wait_ge(h2_written, 16)

            behind = (W - 1 + NB) // W + 1
            assert behind + 2 <= RING and RING % SW == 0 and RING & (RING - 1) == 0

            def gather_h2(i, first, windows=RING):
                for w in range(windows):
                    k = w % SW
                    pool.wait_ge(ld_didx[k], 16 * (i * (RING // SW) + w // SW + 1))
                    pool.sem_inc(pool_tick, 1)
                    if not first:
                        pool.wait_ge(nsum_ready, R * (i * RING + w - RING + behind))
                        pool.sem_inc(pool_tick, 1)
                    for t in range(W):
                        nc.gpsimd.indirect_dma_start(
                            out=h2g[:, w * W + t, :], out_offset=None, in_=h2_rows,
                            in_offset=bass.IndirectOffsetOnAxis(ap=didx[:, k, t, 1:2].bitcast(U32), axis=0)).then_inc(gh[k], 16)
            gather_h2(0, True)
            with pool.Fori(1, TW // RING) as i:
                gather_h2(i, False)
            gather_h2(TW // RING, False, TW % RING)

        @block.scalar
        def _(act):
            act.wait_ge(var_ready, 1)
            nc.scalar.activation(stat[:, 1, :], stat[:, 1, :], ACT.Sqrt).then_inc(std_ready, 1)
            act.wait_ge(h_ready, 1)

            def stage_h(i, k, first):
                if not first:
                    act.wait_ge(hsT_ready, i * 2 + k - 1)
                    act.sem_inc(act_tick, 1)
                nc.scalar.activation(hs[:, k, :].rearrange("p (u f) -> p u f", u=U), h[:, bass.ds((i * 2 + k) * U, U), :], ACT.Copy).then_inc(hs_ready, 1)

            def tables(i, first, last):
                for k in range(2):
                    act.wait_ge(hsT_ready, i * 2 + k + 1)
                    nc.scalar.activation(hT[:, k, :], pb[k][:, 0:P], ACT.Copy).then_inc(hT_ready, 1)
                if not last:
                    for k in range(2):
                        stage_h(i + 1, k, False)
                for k in range(2):
                    act.wait_ge(tab_ready, i * 2 + k + 1)
                    act.sem_inc(act_tick, 1)
                    for n in range(2):
                        nc.scalar.activation(t1[:, bass.ds((i * 2 + k) * U + 2 * n, 2), :],
                                             pb[2 + 2 * k + n][:, :].rearrange("p (u c) -> p u c", u=2)[:, :, 0:P], ACT.Copy)
                    if not first:
                        act.wait_ge(t2_written[k], 16 * i)
                        act.sem_inc(act_tick, 1)
                    for n in range(2):
                        ins = nc.scalar.activation(t2s[:, k, 2 * n:2 * n + 2, :],
                                                   pb[2 + 2 * k + n][:, :].rearrange("p (u c) -> p u c", u=2)[:, :, P:2 * P], ACT.Copy)
                    ins.then_inc(t2s_ready, 1)
            for k in range(2):
                stage_h(0, k, True)
            rounds_of(act, NG // 2, tables)

            act.wait_ge(wf2T_ps, 1)
            nc.scalar.activation(wf2T[:, :], pb[7][0:HID, 0:ACC], ACT.Copy).then_inc(wf2T_ready, 1)
            act.wait_ge(wflow_ps, 1)
            for k in range(2):
                ins = nc.scalar.activation(wflow[:, k, k * HID:(k + 1) * HID], pb[7][0:ACC, 0:HID], ACT.Copy)
            ins.then_inc(wflow_ready, 1)

            def count_src(b, m, first):
                if not first:
                    act.wait_ge(cum_act, b - 1)
                    act.sem_inc(act_tick, 1)
                nc.scalar.activation(junk_of["act"][m], nblk[:, 0, :], ACT.Sign, bias=half_blk[:, bass.ds(b, 1)], scale=-1.0,
                                     accum_out=cum[:, 0, bass.ds(b + 1, 1)]).then_inc(cum_act, 1)
            act.wait_ge(nblk_ready, 1)
            for m in range(2):
                count_src(m, m, True)
            with act.Fori(1, N_ACT // 2) as i:
                for m in range(2):
                    count_src(i * 2 + m, m, False)

            def transposed(i, r):
                v = i * R + r + 1
                act.wait_ge(tp_ready, v)
                nc.scalar.activation(oht[:, r % 2, :, :].rearrange("p u n -> p (u n)"), pb[0][:, :], ACT.Copy)
                nc.scalar.activation(eaT[:, r % 2, :, :].rearrange("p u n -> p (u n)"), pb[1][0:EA + 1, :], ACT.Copy).then_inc(oht_ready, 1)

            def hidden(i, r, first):
                v = i * R + r + 1
                act.wait_ge(pre_ready, v)
                pre = pb[2][:, :].rearrange("p (u c) -> p u c", u=U)
                if not (first and r == 0):
                    act.wait_ge(sum_ready, v - 1)
                nc.scalar.activation(rf[:, :, 0:HID], pre[:, :, 0:HID], ACT.Relu)
                if not first:
                    act.wait_ge(sct[r], 16 * U * i)
                    act.sem_inc(act_tick, 1)
                nc.scalar.copy(rec[:, r, :, HID + 1:REC].bitcast(I32), rec_i[:, r, :, :])
                nc.scalar.activation(rec[:, r, :, 0:HID], pre[:, :, HID:P], ACT.Relu).then_inc(relu_ready, 1)

            def edges(i, first, last):
                for r in range(R):
                    hidden(i, r, first)
                    if r < R - 1:
                        transposed(i, r + 1)
                    elif not last:
                        transposed(i + 1, 0)
            transposed(0, 0)
            rounds(act, edges)

            def record_indices(i, first, last):
                for w in range(SW):
                    act.wait_ge(ld_srec[w], 16 * (i + 1))
                    act.sem_inc(act_tick, 1)
                    for r in range(R):
                        j0 = (i * SW + w) * W + r * U
                        at = four(act, e0[0], j0, W - 1)
                        for u in range(U):
                            ins = nc.scalar.copy(pairs[:, bass.ds(j0 + u, 1), :].rearrange("p a k -> p (a k)"),
                                                 srec[w][:, bass.ds(at[u], 1), HID + 1:REC].bitcast(I32).rearrange("p a k -> p (a k)"))
                        ins.then_inc(pair_ready, 1)
            rounds_of(act, NI // SW, record_indices)

            def nodes(i, first, last):
                for k in range(2):
                    act.wait_ge(accT_ps, i * 2 + k + 1)
                    nc.scalar.activation(accT[:, k, :], pb[k][0:ACC, :], ACT.Copy).then_inc(accT_ready, 1)
                act.wait_ge(node_ps, i + 1)
                nc.scalar.activation(nodeT, pb[2][:, :], ACT.Relu, bias=bn1c[:, :]).then_inc(node_ready, 1)
            rounds_of(act, NG // 2, nodes)
            act.wait_ge(var2_ready, 1)
            nc.scalar.activation(stat[:, 1, :], stat[:, 1, :], ACT.Sqrt).then_inc(std2_ready, 1)

            act.wait_ge(x1_done, NG)
            nc.scalar.activation(acc2[:, :, :], xs[:, :, :], ACT.Copy).then_inc(acc2_set, 1)

        @block.tensor
        def _(pe):
            pe.wait_ge(consts, 1)
            pe.wait_ge(w_in, 16 * N_W)

            def transpose_h(i, k):
                pe.wait_ge(hs_ready, i * 2 + k + 1)
                nc.tensor.transpose(pb[k][:, 0:P], hs[:, k, :], ident[:, :]).then_inc(hsT_ready, 1)

            def tables(i, first, last):
                for k in range(2):
                    if not first:
                        pe.wait_ge(t2s_ready, i * 2 + k - 1)
                        pe.sem_inc(pe_tick, 1)
                    pe.wait_ge(hT_ready, i * 2 + k + 1)
                    for u in range(U):
                        ins = nc.tensor.matmul(pb[2 + 2 * k + u // 2][:, (u % 2) * 2 * P:(u % 2 + 1) * 2 * P], hT[:, k, :], w12[:, u, :],
                                               start=True, stop=True)
                    ins.then_inc(tab_ready, 1)
                if not last:
                    for k in range(2):
                        transpose_h(i + 1, k)
            for k in range(2):
                transpose_h(0, k)
            rounds_of(pe, NG // 2, tables)
            pe.wait_ge(t2s_ready, NG)

            nc.tensor.transpose(pb[7][0:HID, 0:ACC], wf2e[:, :], ident[0:ACC, 0:ACC]).then_inc(wf2T_ps, 1)
            pe.wait_ge(wf2T_ready, 1)
            nc.tensor.matmul(pb[7][0:ACC, 0:HID], wf2T[:, :], wn1[:, :], start=True, stop=True).then_inc(wflow_ps, 1)
            pe.wait_ge(wflow_ready, 1)

            for n, k in enumerate((1, 0)):
                pe.wait_ge(cnt_ready, n + 1)
                nc.tensor.matmul(pb[3][0:NB, 0:1], cum[:, k, 0:NB], ones[0:NP, 0:1], start=True, stop=True)
                nc.tensor.matmul(pb[3][0:NB, 1:2], cum[:, k, 1:NB + 1], ones[0:NP, 0:1], start=True, stop=True).then_inc(n_ready, 1)
                pe.wait_ge(tiles_ready, n + 1)
                nc.tensor.matmul(pb[3][0:NB, 2:3], upto[0:NB, 0:NB], tile_col[:, 3:4], start=True, stop=True).then_inc(tend_ready, 1)
                pe.wait_ge(ge_ready, n + 1)
                for c in range(J // JC):
                    w = n * (J // JC) + c
                    if w > 1:
                        pe.wait_ge(sched_read, w - 1)
                    cols = ge[:, c * JC:(c + 1) * JC]
                    nc.tensor.matmul(pb[sched_bank[w % 2]][:, 0:JC], c128[:, :], cols, start=True, stop=True)
                    nc.tensor.matmul(pb[sched_bank[w % 2] + 1][0:1, 0:JC], slack_h[:, k:k + 1], cols, start=True, stop=True).then_inc(sched_ps, 1)
                if k == 1:
                    nc.tensor.matmul(pb[7][0:NP, 0:NB], ones[0:NP, 0:NP], cum[:, 1, 0:NB], start=True, stop=False)
                    nc.tensor.matmul(pb[7][0:NP, 0:NB], before[0:NP, 0:NP], cnt[:, :], start=False, stop=True).then_inc(fbase_ps, 1)
                    pe.wait_ge(viol_ready, 1)
                    pe.wait_ge(fbase_ready, 1)
                    nc.tensor.matmul(pb[7][0:1, 256:257], viol[:, 2:3], ones[0:NP, 0:1], start=True, stop=True).then_inc(flag_ps, 1)

            pe.wait_ge(flag_ready, 1)
            nc.tensor.matmul(pb[7][:, 0:NB], ones[0:NP, :], cum[:, 0, 0:NB], start=True, stop=True).then_inc(begin_ps, 1)
            q = pb[4][:, 0:(U + 1) * NB].rearrange("p (u b) -> p u b", b=NB)

            def transposes(i, r, very_first=False):
                v = i * R + r + 1
                if not very_first:
                    pe.wait_ge(oht_ready, v - 1)
                    pe.sem_inc(pe_tick, 1)
                pe.wait_ge(ohd_ready, v)
                for u in range(U):
                    nc.tensor.transpose(pb[0][:, u * P:(u + 1) * P], ohd[:, r % 2, u, :], ident[:, :])
                pe.wait_ge(ld_ea[r], 16 * U * (i + 1))
                for u in range(U):
                    ins = nc.tensor.transpose(pb[1][0:EA + 1, u * P:(u + 1) * P], eat[:, r, u, :], ident[:, :])
                ins.then_inc(tp_ready, 1)

            def hidden(i, r):
                v = i * R + r + 1
                at = four(pe, blk[1], i * W + r * U, NB)
                pe.wait_ge(gat[r], 16 * U * (i + 1))
                pe.sem_inc(pe_tick, 1)
                pe.wait_ge(oht_ready, v)
                for u in range(U):
                    p = pb[2][:, u * P:(u + 1) * P]
                    nc.tensor.matmul(p, ident[:, :], g2[:, r, u, :], start=True, stop=False)
                    nc.tensor.matmul(p, eaT[:, r % 2, u, :], wee[:, :], start=False, stop=False)
                    ins = nc.tensor.matmul(p, oht[:, r % 2, u, :], t1[:, bass.ds(at[u], 1), :].rearrange("p a c -> p (a c)"), start=False, stop=True)
                ins.then_inc(pre_ready, 1)

            def counts(i, r, first):
                v = i * R + r + 1
                o = ohs[:, r % 2, :, :]
                if not (first and r == 0):
                    pe.wait_ge(q_read, v - 1)
                    pe.sem_inc(pe_tick, 1)
                pe.wait_ge(ohs_ready, v)
                nc.tensor.matmul(q[:, 0:U, :], before_h[:, :], o, start=True, stop=False)
                nc.tensor.matmul(q[:, U, :], ones_h[:, :], o[:, 0, :], start=False, stop=False)
                nc.tensor.matmul(q[:, 1:U, :], ones_h[:, :], bcast_mid(o[:, 0, :], U - 1), start=False, stop=False)
                for c in range(1, U):
                    ins = nc.tensor.matmul(q[:, c + 1:U + 1, :], ones_h[:, :], bcast_mid(o[:, c, :], U - c), start=False, stop=c == U - 1)
                ins.then_inc(q_ready, 1)

            def sums(i, r, first):
                v = i * R + r + 1
                if not (first and r == 0):
                    pe.wait_ge(acc_done, v - 1)
                    pe.sem_inc(pe_tick, 1)
                pe.wait_ge(relu_ready, v)
                for u in range(U):
                    ins = nc.tensor.matmul(pb[3][:, u * ACC:(u + 1) * ACC], ohd[:, r % 2, u, :], rf[:, u, :], start=True, stop=True)
                ins.then_inc(sum_ready, 1)

            def edges(i, first, last):
                for r in range(R):
                    hidden(i, r)
                    if r < R - 1:
                        transposes(i, r + 1)
                    elif not last:
                        transposes(i + 1, 0)
                    counts(i, r, first)
                    sums(i, r, first)
            transposes(0, 0, True)
            rounds(pe, edges)

            def sum_records(i, first, last):
                for w in range(SW):
                    at = window_of(pe, e0[0], (i * SW + w) * W, W - 1)
                    for r in range(R):
                        v = (i * SW + w) * R + r + 1
                        pe.wait_ge(soh_ready, v)
                        pe.sem_inc(pe_tick, 1)
                        for u in range(U):
                            ins = nc.tensor.matmul(s_bank[r][:, u * ACC:(u + 1) * ACC], s_oh[r][:, u, :],
                                                   srec[w][:, bass.ds(at[r * U + u], 1), 0:ACC].rearrange("p a c -> p (a c)"), start=True, stop=True)
                        ins.then_inc(ssum_ready, 1)
            pe.wait_ge(relu_ready, NI * R)
            pe.wait_ge(acc_done, NI * R)
            rounds_of(pe, NI // SW, sum_records)

            nc.tensor.matmul(pb[7][:, 0:D], ones[0:1, :], bn2r[:, :], start=True, stop=True).then_inc(b1_ready, 1)

            def transpose_sums(i, k, first):
                if not first:
                    pe.wait_ge(accT_ready, i * 2 + k - 1)
                    pe.sem_inc(pe_tick, 1)
                pe.wait_ge(accs_ready, i * 2 + k + 1)
                for u in range(U):
                    ins = nc.tensor.transpose(pb[k][0:ACC, u * P:(u + 1) * P], accs[:, k, u, :], ident[:, :])
                ins.then_inc(accT_ps, 1)

            def nodes(i, first, last):
                if not first:
                    pe.wait_ge(node_ready, i)
                    pe.sem_inc(pe_tick, 1)
                for k in range(2):
                    pe.wait_ge(accT_ready, i * 2 + k + 1)
                    pe.sem_inc(pe_tick, 1)
                    ins = nc.tensor.matmul(pb[2][:, :], wflow[:, k, :], accT[:, k, :], start=k == 0, stop=k == 1)
                ins.then_inc(node_ps, 1)
                if not last:
                    for k in range(2):
                        transpose_sums(i + 1, k, False)
                if not first:
                    pe.wait_ge(x1_done, i * 2)
                    pe.sem_inc(pe_tick, 1)
                pe.wait_ge(node_ready, i + 1)
                for u in range(U):
                    ins = nc.tensor.matmul(pb[5][:, u * 2 * D:(u + 1) * 2 * D], nodeT[:, u * P:(u + 1) * P],
                                           wn2[:, :, :].rearrange("p k f -> p (k f)"), start=True, stop=True)
                ins.then_inc(outp_ps, 1)
            for k in range(2):
                transpose_sums(0, k, True)
            rounds_of(pe, NG // 2, nodes)

            pe.wait_ge(slots_ready, 1)

            def sum_neighbours(i, gathers=SW):
                for w in range(SW):
                    at = window_of(pe, ring_slot, (i * SW + w) * W, RING * W - 1)
                    if w < gathers:
                        pe.wait_ge(gh[w], 16 * W * (i + 1))
                        pe.sem_inc(pe_tick, 1)
                    for r in range(R):
                        v = (i * SW + w) * R + r + 1
                        pe.wait_ge(noh_ready, v)
                        pe.sem_inc(pe_tick, 1)
                        for u in range(U):
                            ins = nc.tensor.matmul(s_bank[r][:, u * D:(u + 1) * D], s_oh[r][:, u, :],
                                                   h2g[:, bass.ds(at[r * U + u], 1), :].rearrange("p a f -> p (a f)"), start=True, stop=True)
                        ins.then_inc(nsum_ready, 1)
            sum_neighbours(0)
            with pe.Fori(1, TW // SW) as i:
                sum_neighbours(i)
            for i in range(TW // SW, NI // SW):
                sum_neighbours(i, max(0, TW - i * SW))

        @block.vector
        def _(dve):
            own = Chain(dve, dve_own)

            def centre(links, src, cols):
                mean = stat[:, 0, cols]
                links.step(nc.vector.reduce_sum(mean, src[:, cols, :], axis=AX))
                links.step(nc.vector.tensor_scalar(mean, mean, 1.0 / D, None, ALU.mult))
                links.step(nc.vector.tensor_tensor(h[:, cols, :], src[:, cols, :], bcast(mean, D), ALU.subtract))
                links.step(nc.vector.tensor_tensor(lnt[:, cols, :], h[:, cols, :], h[:, cols, :], ALU.mult))
                links.step(nc.vector.reduce_sum(stat[:, 1, cols], lnt[:, cols, :], axis=AX))

            def scale_relu(var_sem, std_sem):
                nc.vector.tensor_scalar(stat[:, 1, :], stat[:, 1, :], 1.0 / D, 1e-5, ALU.mult, ALU.add).then_inc(var_sem, 1)
                dve.wait_ge(std_sem, 1)
                own.step(nc.vector.reciprocal(stat[:, 0, :], stat[:, 1, :]))
                own.step(nc.vector.tensor_tensor(h[:, :, :], h[:, :, :], bcast(stat[:, 0, :], D), ALU.mult))
                return nc.vector.tensor_scalar(h[:, :, :], h[:, :, :], 0.0, None, ALU.max)

            dve.wait_ge(x_in, 32)
            centre(own, xs, slice(0, NBP))
            scale_relu(var_ready, std_ready).then_inc(h_ready, 1)

            dve.wait_ge(h_ready, 1)
            dve.wait_ge(nat_in, 32)
            dve.wait_ge(consts, 1)
            for k in (1, 0):
                own.step(nc.vector.tensor_scalar(blk_i, nat[:, :, k], 7, None, ALU.arith_shift_right))
                own.step(nc.vector.tensor_copy(nblk[:, k, :], blk_i))
            nc.vector.tensor_scalar(half_blk[:, :], iota_blk1[0:NP, 0:N_ACT], 0.5, None, ALU.subtract).then_inc(nblk_ready, 1)
            own.link(nc.vector.memset(row_nextf[:, :], float(FAR)))
            own.step(nc.vector.tensor_scalar(row_nexti[0:NP - 1, :], row_next[0:NP - 1, 1:2], 7, None, ALU.arith_shift_right))
            own.step(nc.vector.tensor_copy(row_nextf[0:NP - 1, :], row_nexti[0:NP - 1, :]))
            own.step(nc.vector.tensor_tensor(junk_d[:, 0:NC - 1], nblk[:, 1, 1:NC], nblk[:, 1, 0:NC - 1], ALU.is_lt))
            own.step(nc.vector.reduce_sum(viol[:, 0:1], junk_d[:, 0:NC - 1], axis=AX))
            own.step(nc.vector.tensor_tensor(viol[:, 1:2], row_nextf[:, :], nblk[:, 1, NC - 1:NC], ALU.is_lt))
            nc.vector.tensor_tensor(viol[:, 2:3], viol[:, 0:1], viol[:, 1:2], ALU.add).then_inc(viol_ready, 1)

            def count(k, b0, b1, before_):
                def one(b, m, first):
                    if not first:
                        dve.wait_ge(cum_ready, b + (before_ - b0 - 1))
                    nc.vector.tensor_scalar(junk_of["dve"][m], nblk[:, k, :], iota_blk1[0:NP, bass.ds(b, 1)], 0.0, ALU.is_lt, ALU.add,
                                            accum_out=cum[:, k, bass.ds(b + 1, 1)]).then_inc(cum_ready, 1)
                for m in range(2):
                    one(b0 + m, m, True)
                with dve.Fori(1, (b1 - b0) // 2) as i:
                    for m in range(2):
                        one(i * 2 + b0 + m, m, False)
                dve.wait_ge(cum_ready, before_ + b1 - b0)

            for n, k in enumerate((1, 0)):
                if k == 1:
                    count(k, 0, NB, 0)
                    nc.vector.tensor_tensor(cnt[:, :], cum[:, 1, 1:NB + 1], cum[:, 1, 0:NB], ALU.subtract).then_inc(cnt_ready, 1)
                else:
                    count(k, N_ACT, NB, NB)
                    dve.wait_ge(cum_act, N_ACT)
                    c = cum[:, 0, 1:N_ACT + 1]
                    nc.vector.tensor_scalar(c, c, 0.5, NC / 2, ALU.mult, ALU.add).then_inc(cnt_ready, 1)
                dve.wait_ge(n_ready, n + 1)
                own.step(nc.vector.tensor_copy(edge_col[:, 0:2], pb[3][0:NB, 0:2]))
                own.link(nc.vector.tensor_scalar(edge_col[:, 2:3], edge_col[:, 1:2], float(P - 1), None, ALU.add))
                own.link(nc.vector.tensor_tensor(edge_col[:, 3:4], edge_col[:, 1:2], edge_col[:, 0:1], ALU.is_gt))
                own.wait()
                own.step(nc.vector.tensor_copy(edge_coli[:, :], edge_col[:, 0:3]))
                own.step(nc.vector.tensor_scalar(edge_coli[:, :], edge_coli[:, :], 7, None, ALU.arith_shift_right))
                own.step(nc.vector.tensor_copy(tile_col[:, 0:3], edge_coli[:, :]))
                own.step(nc.vector.tensor_tensor(tile_col[:, 3:4], tile_col[:, 2:3], tile_col[:, 0:1], ALU.subtract))
                nc.vector.tensor_tensor(tile_col[:, 3:4], tile_col[:, 3:4], edge_col[:, 3:4], ALU.mult).then_inc(tiles_ready, 1)
                dve.wait_ge(tiles_ready, n + 1)
                own.step(nc.vector.tensor_tensor(slack[:, k:k + 1], tile_col[:, 1:2], tile_col[:, 0:1], ALU.subtract))
                own.step(nc.vector.tensor_tensor(slack[:, k:k + 1], slack[:, k:k + 1], tile_col[:, 3:4], ALU.subtract))
                own.link(nc.vector.tensor_scalar(slack_h[:, k:k + 1], slack[:, k:k + 1], float(P), None, ALU.mult))
                dve.wait_ge(tend_ready, n + 1)
                own.step(nc.vector.tensor_copy(tend[:, k:k + 1], pb[3][0:NB, 2:3]))
                nc.vector.tensor_scalar(ge[:, :], jrow[:, :], tend[:, k:k + 1], None, ALU.is_ge).then_inc(ge_ready, 1)
                for c in range(J // JC):
                    dve.wait_ge(sched_ps, n * (J // JC) + c + 1)
                    s = slice(c * JC, (c + 1) * JC)
                    bank = sched_bank[(n * (J // JC) + c) % 2]
                    nc.vector.tensor_copy(base_row[k][:, s], pb[bank][:, 0:JC])
                    nc.vector.tensor_scalar(blk[k][:, s], pb[bank][0:1, 0:JC], 1.0 / P, None, ALU.mult)
                    nc.vector.tensor_copy(e0f[:, s], pb[bank + 1][0:1, 0:JC]).then_inc(sched_read, 1)
                dve.wait_ge(sched_read, (n + 1) * (J // JC))
                own.step(nc.vector.scalar_tensor_tensor(e0f[:, :], jrow[0:1, :], float(P), e0f[:, :], op0=ALU.mult, op1=ALU.add))
                top = float(EP - W * P)
                if k == 1:
                    nc.vector.tensor_scalar(e0[k][:, :], e0f[:, :], top, None, ALU.min).then_inc(sched_done, 1)
                else:
                    own.step(nc.vector.tensor_scalar(e0f[:, :], e0f[:, :], top, None, ALU.min))
                    steps = e0f.rearrange("p (i s) -> p i s", s=W)
                    first_ = steps[:, :, 0]
                    own.link(nc.vector.tensor_copy(window[:, :], first_))
                    own.step(nc.vector.tensor_tensor(steps[:, :, 1:W], steps[:, :, 1:W], bcast(first_, W - 1), ALU.subtract))
                    own.step(nc.vector.tensor_scalar(steps[:, :, 0:1], steps[:, :, 0:1], 0.0, None, ALU.mult))
                    nc.vector.tensor_scalar(e0[k][:, :], e0f[:, :], 1.0 / P, None, ALU.mult).then_inc(sched_done, 1)
                if k == 1:
                    dve.wait_ge(fbase_ps, 1)
                    nc.vector.tensor_copy(fb_base, pb[7][0:NP, 0:NB]).then_inc(fbase_ready, 1)
                    dve.wait_ge(flag_ps, 1)
                    nc.vector.tensor_copy(flag[:, :], pb[7][0:1, 256:257]).then_inc(flag_ready, 1)
            dve.wait_ge(rearranged, 1)
            dve.wait_ge(sched_read, 2 * (J // JC))
            own.step(nc.vector.memset(acc[:, :, :], 0.0))
            dve.wait_ge(sched_done, 2)

            dve.wait_ge(begin_ps, 1)
            own.step(nc.vector.tensor_copy(q_row[:, 0, :], pb[7][:, 0:NB]))

            chain = Chain(dve, dve_d)
            q = pb[4][:, 0:(U + 1) * NB].rearrange("p (u b) -> p u b", b=NB)

            def small_of(r):
                return [small[:, r % 2, m, :] for m in range(7)]

            def dst_row(i, r):
                dloc = small_of(r)[0]
                dve.wait_ge(ld_sd[r], 16 * U * (i + 1))
                floats = chain.link(nc.vector.tensor_copy(sdf[:, r % 2, :, :], rec_i[:, r, :, :]))
                blocks = chain.link(nc.vector.tensor_scalar(sblk[:, r % 2, :], rec_i[:, r, :, 0], 7, None, ALU.arith_shift_right))
                chain.wait(floats)
                row = chain.link(nc.vector.tensor_tensor(dloc, sdf[:, r % 2, :, 1], base_row[1][:, bass.ds(i * W + r * U, U)], ALU.subtract))
                return row

            def dst_one_hot(r, row):
                dloc, clamp, valid, key, off, skey, _ = small_of(r)
                chain.wait(row)
                nc.vector.tensor_tensor(ohd[:, r % 2, :, :], bcast_mid(iota128[:, :], U), bcast(dloc, P), ALU.is_equal).then_inc(ohd_ready, 1)
                clamped = chain.link(nc.vector.tensor_scalar(clamp, dloc, 0.0, float(P - 1), ALU.max, ALU.min))
                chain.link(nc.vector.tensor_scalar(skey, sblk[:, r % 2, :], 1.0, None, ALU.add))
                return clamped

            def src_one_hot(r, clamped):
                dloc, clamp, valid, key, off, skey, _ = small_of(r)
                chain.wait(clamped)
                chain.step(nc.vector.tensor_tensor(valid, clamp, dloc, ALU.is_equal))
                keyed = chain.link(nc.vector.tensor_tensor(key, skey, valid, ALU.mult))
                chain.link(nc.vector.tensor_scalar(off, valid, -BIG, BIG, ALU.mult, ALU.add))
                chain.wait(keyed)
                nc.vector.tensor_tensor(ohs[:, r % 2, :, :], bcast_mid(iota_blk1[:, :], U), bcast(key, NB), ALU.is_equal).then_inc(ohs_ready, 1)

            def add_step(dst, at, src, width, u):
                to = dst[:, bass.ds(at[u], 1), :].rearrange("p a c -> p (a c)")
                return nc.vector.tensor_tensor(to, to, src[:, u * width:(u + 1) * width], ALU.add)

            def positions(i, r, first):
                v = i * R + r + 1
                off, p = small_of(r)[4], small_of(r)[6]
                if not first:
                    dve.wait_ge(sct[r], 16 * U * i)
                    dve.sem_inc(dve_tick, 1)
                dve.wait_ge(q_ready, v)
                placed = chain.link(nc.vector.tensor_tensor(prod[:, :, :], q[:, 0:U, :], bcast_mid(q_row[:, r % 2, :], U), ALU.add))
                nc.vector.tensor_tensor(q_row[:, (r + 1) % 2, :], q_row[:, r % 2, :], q[:, U, :], ALU.add).then_inc(q_read, 1)
                chain.wait(placed)
                chain.link(nc.vector.tensor_tensor(prod[:, :, :], prod[:, :, :], ohs[:, r % 2, :, :], ALU.mult))
                chain.wait()
                chain.step(nc.vector.reduce_sum(p, prod[:, :, :], axis=AX))
                nc.vector.tensor_tensor(pos[:, r, :], p, off, ALU.add).then_inc(pos_ready, 1)

            def add_and_prepare(i, r, first, ahead):
                v = i * R + r + 1
                at = four(dve, blk[1], i * W + r * U, NB)
                if not (first and r == 0):
                    dve.wait_ge(acc_done, v - 1)
                    dve.sem_inc(dve_tick, 1)
                dve.wait_ge(sum_ready, v)
                added = chain.link(add_step(acc, at, pb[3], ACC, 0))
                row = dst_row(*ahead) if ahead else None
                chain.wait(added)
                added = chain.link(add_step(acc, at, pb[3], ACC, 1))
                clamped = dst_one_hot(ahead[1], row) if ahead else None
                chain.wait(added)
                added = chain.link(add_step(acc, at, pb[3], ACC, 2))
                if ahead:
                    src_one_hot(ahead[1], clamped)
                chain.wait(added)
                add_step(acc, at, pb[3], ACC, 3).then_inc(acc_done, 1)

            assert U == 4
            per = R * (8 + 3 + 3)

            def edges(i, first, last):
                chain.n, chain.base = FRONT, i * per
                for r in range(R):
                    positions(i, r, first)
                    ahead = (i, r + 2) if r < R - 2 else None if last else (i + 1, r + 2 - R)
                    add_and_prepare(i, r, first, ahead)
                assert last or chain.n == FRONT + per, (chain.n, FRONT, per)
            for r in range(2):
                src_one_hot(r, dst_one_hot(r, dst_row(0, r)))
            FRONT = chain.n
            assert FRONT == 16
            rounds(dve, edges)

            schain = Chain(dve, dve_s)
            dve.wait_ge(pre_ready, NI * R)
            AHEAD = R - 1

            def src_rows(i, w):
                cols = bass.ds((i * SW + w) * W, W)
                dve.wait_ge(pair_ready, (i * SW + w + 1) * R)
                dve.sem_inc(dve_tick, 1)
                return schain.link(nc.vector.tensor_tensor(pairs[:, cols, 0], pairs[:, cols, 0], base_row[0][:, cols], ALU.subtract))

            def src_row_one_hot(i, w, r, u):
                col = bass.ds((i * SW + w) * W + r * U + u, 1)
                ins = nc.vector.tensor_tensor(s_oh[r][:, u, :], iota128[:, :], pairs[:, col, 0].broadcast_to([P, P]), ALU.is_equal)
                if u == U - 1:
                    ins.then_inc(soh_ready, 1)

            def records_summed(i, first, last):
                schain.n = 0
                added = None
                for w in range(SW):
                    at = window_of(dve, blk[0], (i * SW + w) * W, NB)
                    for r in range(R):
                        v = (i * SW + w) * R + r + 1
                        window = (i, w) if r < R - AHEAD else (i, w + 1) if w < SW - 1 else None if last else (i + 1, 0)
                        later = (r + AHEAD) % R
                        rows = src_rows(*window) if window and later == 0 else None
                        for u in range(U):
                            if added is not None:
                                schain.wait(added)
                            if u == 0:
                                dve.wait_ge(ssum_ready, v)
                            added = schain.link(add_step(acc, at[r * U:(r + 1) * U], s_bank[r], ACC, u))
                            if window:
                                if u == 0 and rows is not None:
                                    schain.wait(rows)
                                src_row_one_hot(*window, later, u)
                schain.wait()
                if not last:
                    dve.sem_clear(dve_s)
            schain.wait(src_rows(0, 0))
            dve.sem_clear(dve_s)
            for r in range(AHEAD):
                for u in range(U):
                    src_row_one_hot(0, 0, r, u)
            rounds_of(dve, NI // SW, records_summed)

            own.step(nc.vector.tensor_scalar(window[:, :], window[:, :], 7, None, ALU.arith_shift_right))
            own.link(nc.vector.tensor_copy(e0f[:, :], e0[0]))
            own.step(nc.vector.tensor_copy(window_f[:, :], window[:, :]))
            tile_f = e0f.rearrange("p (i s) -> p i s", s=W)
            own.step(nc.vector.tensor_tensor(tile_f, tile_f, bcast(window_f[:, :], W), ALU.add))
            own.step(nc.vector.tensor_copy(ring_slot, e0f[:, :]))
            nc.vector.tensor_scalar(ring_slot, ring_slot, RING * W - 1, None, ALU.bitwise_and).then_inc(slots_ready, 1)

            def stage_sums(i, k, first):
                if not first:
                    dve.wait_ge(accT_ps, i * 2 + k - 1)
                    dve.sem_inc(dve_tick, 1)
                nc.vector.tensor_copy(accs[:, k, :, :], acc[:, bass.ds((i * 2 + k) * U, U), :]).then_inc(accs_ready, 1)
            for k in range(2):
                stage_sums(0, k, True)
            dve.wait_ge(b1_ready, 1)
            own.step(nc.vector.tensor_copy(bn2b[:, :], pb[7][:, 0:D]))
            own.step(nc.vector.tensor_tensor(xs[:, :, :], xs[:, :, :], bcast_mid(bn2b[:, :], NBP), ALU.add))

            nchain = Chain(dve, dve_n, dve_tick)

            def centre_x1(i):
                nchain.n, nchain.base = 0, i * 5
                dve.wait_ge(x1_done, (i + 1) * 2)
                dve.sem_inc(dve_tick, 1)
                centre(nchain, xs, bass.ds(i * 2 * U, 2 * U))
                assert nchain.n == 5

            def nodes(i, first, last):
                if not last:
                    for k in range(2):
                        stage_sums(i + 1, k, False)
                if not first:
                    centre_x1(i - 1)
                dve.wait_ge(outp_ps, i + 1)
                dve.sem_inc(dve_tick, 1)
                for k in range(2):
                    to = xs[:, bass.ds((i * 2 + k) * U, U), :]
                    nc.vector.tensor_tensor(to, to, pb[5][:, 0:U * 2 * D].rearrange("p (u k f) -> p u k f", u=U, k=2)[:, :, k, :], ALU.add).then_inc(x1_done, 1)
            rounds_of(dve, NG // 2, nodes)
            centre_x1(NG // 2 - 1)
            scale_relu(var2_ready, std2_ready).then_inc(h2_ready, 1)

            gchain = Chain(dve, dve_g)
            dve.wait_ge(acc2_set, 1)

            def neighbour_one_hot(i, w, r, u):
                col = bass.ds((i * SW + w) * W + r * U + u, 1)
                ins = nc.vector.tensor_tensor(s_oh[r][:, u, :], iota128[:, :], pairs[:, col, 0].broadcast_to([P, P]), ALU.is_equal)
                if u == U - 1:
                    ins.then_inc(noh_ready, 1)

            def neighbours(i, first, last):
                gchain.n = 0
                added = None
                for w in range(SW):
                    at = window_of(dve, blk[0], (i * SW + w) * W, NB)
                    for r in range(R):
                        window = (i, w) if r < R - AHEAD else (i, w + 1) if w < SW - 1 else None if last else (i + 1, 0)
                        for u in range(U):
                            if added is not None:
                                gchain.wait(added)
                            if u == 0:
                                dve.wait_ge(nsum_ready, (i * SW + w) * R + r + 1)
                            added = gchain.link(add_step(acc2, at[r * U:(r + 1) * U], s_bank[r], D, u))
                            if window:
                                neighbour_one_hot(*window, (r + AHEAD) % R, u)
                gchain.wait()
                if not last:
                    dve.sem_clear(dve_g)
            for r in range(AHEAD):
                for u in range(U):
                    neighbour_one_hot(0, 0, r, u)
            rounds_of(dve, NI // SW, neighbours)
            dve.sem_inc(all_added, 1)


N_W = 16 + 4 + 8


def kernel(**inputs):
    import numpy as np
    import concourse.bacc as bacc
    from concourse.bass_utils import run_bass_kernel_spmd

    nc = bacc.Bacc("TRN2", target_bir_lowering=False, num_devices=1)
    laid = {"x": inputs["x"], "sd": np.stack([inputs["src"], inputs["dst"]], axis=1), "ea": inputs["edge_attr_16"]}
    for name in ("Wf1", "bf1", "Wf2", "bf2", "Wn1", "bn1", "Wn2", "bn2"):
        laid[name] = inputs[f"L0_gnn_{name}"]
    arrays, args = {}, []
    for name, a in laid.items():
        a = np.ascontiguousarray(a)
        arrays[f"in_{name}"] = a
        args.append(nc.dram_tensor(f"in_{name}", a.shape, mybir.dt.from_np(a.dtype), kind="ExternalInput").ap())
    args.append(nc.dram_tensor("out_x", (N, D), F32, kind="ExternalOutput").ap())
    build(nc, *args)
    r = run_bass_kernel_spmd(nc, [arrays], core_ids=[0])
    return r.results[0]["out_x"]
```
